# Optimizing a Trainium2 kernel written in Bass

```python
import numpy as np
import jax
import jax.numpy as jnp

def _softmax(x, axis=-1):
    return jax.nn.softmax(x, axis=axis)

def _gelu(x):
    return jax.nn.gelu(x, approximate=True)

def _silu(x):
    return jax.nn.silu(x)

def _sigmoid(x):
    return jax.nn.sigmoid(x)

def _layernorm(x, axis=-1, eps=1e-05):
    m = jnp.mean(x, axis=axis, keepdims=True)
    v = jnp.var(x, axis=axis, keepdims=True)
    return (x - m) / jnp.sqrt(v + eps)

def _scatter_add(tgt, idx, src, axis=0):
    return tgt.at[idx].add(src)

def _segment_sum(src, seg, n):
    return jax.ops.segment_sum(src, seg, n)
kernel_name = 'mk_decoder_postln_d1_seqx_r8_f05ee3'

def setup_inputs(seed: int=0):
    np.random.seed(seed)
    _w = jnp.asarray

    def _rec_inputs():
        import jax
        import jax.numpy as jnp
        _rk = jax.random.key(seed)
        x = 0.0003765 + 1 * jax.random.normal(jax.random.fold_in(_rk, 1), (8, 128, 256), jnp.float32)
        _lenS = 128 - jax.random.randint(jax.random.fold_in(_rk, 7), (8,), 0, max(1, 128 // 4) + 1, jnp.int32)
        _lenS2 = 128 - jax.random.randint(jax.random.fold_in(_rk, 8), (8,), 0, max(1, 128 // 4) + 1, jnp.int32)
        _ctx_2048P = jax.random.normal(jax.random.fold_in(_rk, 11), (8, 16, 256), jnp.float32)
        _ctx_2048c = jax.random.dirichlet(jax.random.fold_in(_rk, 511), 0.3 * jnp.ones((16,), jnp.float32), (8, 128))
        _ctx_2048t = jnp.einsum('bsk,bkd->bsd', _ctx_2048c, _ctx_2048P)
        _ctx_2048t = _ctx_2048t * jax.lax.rsqrt(jnp.mean(jnp.square(_ctx_2048t)) + 1e-12) * 0.953939
        ctx_2048 = -0.000292821 + 1.00034 * (_ctx_2048t + 0.3 * jax.random.normal(jax.random.fold_in(_rk, 611), (8, 128, 256), jnp.float32))
        return (x, ctx_2048)
    x, ctx_2048 = _rec_inputs()

    def _L0_attn_setup():
        import jax, jax.numpy as jnp
        import numpy as np
        D_MODEL = 256
        N_HEADS = 16
        D_HEAD = D_MODEL // N_HEADS
        B, S = (2, 256)
        EPS = 1e-05

        def _mhsa(X, ln_g, ln_b, Wq, bq, Wk, bk, Wv, bv, Wo, bo):
            n_ctx = X.shape[-2]
            mu = jnp.mean(X, axis=-1, keepdims=True)
            var = jnp.mean(jnp.square(X - mu), axis=-1, keepdims=True)
            Xn = (X - mu) * jax.lax.rsqrt(var + EPS) * ln_g + ln_b

            def split_heads(t):
                return t.reshape(t.shape[:-1] + (N_HEADS, D_HEAD)).swapaxes(-2, -3)
            Q = split_heads(Xn @ Wq + bq)
            K = split_heads(Xn @ Wk + bk)
            V = split_heads(Xn @ Wv + bv)
            scores = jnp.einsum('bhqd,bhkd->bhqk', Q, K) / jnp.sqrt(jnp.float32(D_HEAD))
            causal = jnp.tril(jnp.ones((n_ctx, n_ctx), dtype=bool))
            scores = jnp.where(causal, scores, jnp.float32(-jnp.inf))
            A = jax.nn.softmax(scores, axis=-1)
            AV = jnp.einsum('bhqk,bhkd->bhqd', A, V)
            AV = AV.swapaxes(-2, -3).reshape(X.shape[:-1] + (D_MODEL,))
            return AV @ Wo + bo
        key = jax.random.key(seed)
        ks = jax.random.split(key, 10)
        sd = 1.0 / np.sqrt(D_MODEL)
        inp = {'X': jax.random.normal(ks[0], (B, S, D_MODEL), dtype=jnp.float32), 'ln_g': jnp.ones((D_MODEL,), jnp.float32), 'ln_b': jnp.zeros((D_MODEL,), jnp.float32), 'Wq': jax.random.uniform(ks[1], (D_MODEL, D_MODEL), jnp.float32, -sd, sd), 'bq': jax.random.uniform(ks[2], (D_MODEL,), jnp.float32, -sd, sd), 'Wk': jax.random.uniform(ks[3], (D_MODEL, D_MODEL), jnp.float32, -sd, sd), 'bk': jax.random.uniform(ks[4], (D_MODEL,), jnp.float32, -sd, sd), 'Wv': jax.random.uniform(ks[5], (D_MODEL, D_MODEL), jnp.float32, -sd, sd), 'bv': jax.random.uniform(ks[6], (D_MODEL,), jnp.float32, -sd, sd), 'Wo': jax.random.uniform(ks[7], (D_MODEL, D_MODEL), jnp.float32, -sd, sd), 'bo': jax.random.uniform(ks[8], (D_MODEL,), jnp.float32, -sd, sd)}
        return inp
    _L0_attn_all = _L0_attn_setup()
    _L0_attn_in = {k: v for k, v in _L0_attn_all.items() if k in ('ln_g', 'ln_b', 'Wq', 'bq', 'Wk', 'bk', 'Wv', 'bv', 'Wo', 'bo')}
    del _L0_attn_all

    def _L0_xattn_setup():
        import jax, jax.numpy as jnp
        import numpy as np
        key = jax.random.key(seed)
        k1, k2, k3, k4, k5 = jax.random.split(key, 5)
        B, D_MODEL, L = (2, 128, 256)
        HEAD_DIM = 8
        H = D_MODEL // HEAD_DIM
        return {'k': jax.random.normal(k1, (B, D_MODEL, L), dtype=jnp.float32), 'v': jax.random.normal(k2, (B, D_MODEL, L), dtype=jnp.float32), 'q': jax.random.normal(k3, (B, D_MODEL, L), dtype=jnp.float32), 'ssm_kernel': jax.random.normal(k4, (H, L), dtype=jnp.float32), 'D': jax.random.normal(k5, (H,), dtype=jnp.float32), 'head_dim': HEAD_DIM}
    _L0_xattn_all = _L0_xattn_setup()
    _L0_xattn_in = {k: v for k, v in _L0_xattn_all.items() if k in ('ssm_kernel', 'D')}
    del _L0_xattn_all

    def _L0_ffn_setup():
        import jax, jax.numpy as jnp
        import numpy as np
        HIDDEN = 256
        INTER = 1024
        RETRIEVAL = 128
        NUM_EXPERTS = 512
        NUM_KEYS = 64
        TOP_K = 8
        B, S = (4, 256)
        key = jax.random.key(seed)
        ks = jax.random.split(key, 8)
        sc = 0.02
        return {'hidden_states': jax.random.normal(ks[0], (B, S, HIDDEN), jnp.float32), 'W_q': jax.random.normal(ks[1], (HIDDEN, RETRIEVAL), jnp.float32) * sc, 'keys': jax.random.normal(ks[2], (2, RETRIEVAL // 2, NUM_KEYS), jnp.float32) * sc, 'down_embed': jax.random.normal(ks[3], (NUM_EXPERTS, HIDDEN), jnp.float32) * sc, 'up_embed': jax.random.normal(ks[4], (NUM_EXPERTS, HIDDEN), jnp.float32) * sc, 'gate_w': jax.random.normal(ks[5], (HIDDEN, INTER), jnp.float32) * sc, 'up_w': jax.random.normal(ks[6], (HIDDEN, INTER), jnp.float32) * sc, 'down_w': jax.random.normal(ks[7], (INTER, HIDDEN), jnp.float32) * sc}
    _L0_ffn_all = _L0_ffn_setup()
    _L0_ffn_in = {k: v for k, v in _L0_ffn_all.items() if k in ('W_q', 'keys', 'down_embed', 'up_embed', 'gate_w', 'up_w', 'down_w')}
    del _L0_ffn_all
    return {'x': x, 'ctx_2048': ctx_2048, 'L0_attn_ln_g': _L0_attn_in['ln_g'], 'L0_attn_ln_b': _L0_attn_in['ln_b'], 'L0_attn_Wq': _L0_attn_in['Wq'], 'L0_attn_bq': _L0_attn_in['bq'], 'L0_attn_Wk': _L0_attn_in['Wk'], 'L0_attn_bk': _L0_attn_in['bk'], 'L0_attn_Wv': _L0_attn_in['Wv'], 'L0_attn_bv': _L0_attn_in['bv'], 'L0_attn_Wo': _L0_attn_in['Wo'], 'L0_attn_bo': _L0_attn_in['bo'], 'L0_xattn_ssm_kernel': _L0_xattn_in['ssm_kernel'], 'L0_xattn_D': _L0_xattn_in['D'], 'L0_ffn_W_q': _L0_ffn_in['W_q'], 'L0_ffn_keys': _L0_ffn_in['keys'], 'L0_ffn_down_embed': _L0_ffn_in['down_embed'], 'L0_ffn_up_embed': _L0_ffn_in['up_embed'], 'L0_ffn_gate_w': _L0_ffn_in['gate_w'], 'L0_ffn_up_w': _L0_ffn_in['up_w'], 'L0_ffn_down_w': _L0_ffn_in['down_w']}

def reference(x, ctx_2048, L0_attn_ln_g, L0_attn_ln_b, L0_attn_Wq, L0_attn_bq, L0_attn_Wk, L0_attn_bk, L0_attn_Wv, L0_attn_bv, L0_attn_Wo, L0_attn_bo, L0_xattn_ssm_kernel, L0_xattn_D, L0_ffn_W_q, L0_ffn_keys, L0_ffn_down_embed, L0_ffn_up_embed, L0_ffn_gate_w, L0_ffn_up_w, L0_ffn_down_w):
    import jax
    import jax.numpy as jnp

    def _L0_attn_ref(X, ln_g, ln_b, Wq, bq, Wk, bk, Wv, bv, Wo, bo):
        import jax, jax.numpy as jnp
        import numpy as np
        D_MODEL = 256
        N_HEADS = 16
        D_HEAD = D_MODEL // N_HEADS
        B, S = (2, 256)
        EPS = 1e-05

        def _mhsa(X, ln_g, ln_b, Wq, bq, Wk, bk, Wv, bv, Wo, bo):
            n_ctx = X.shape[-2]
            mu = jnp.mean(X, axis=-1, keepdims=True)
            var = jnp.mean(jnp.square(X - mu), axis=-1, keepdims=True)
            Xn = (X - mu) * jax.lax.rsqrt(var + EPS) * ln_g + ln_b

            def split_heads(t):
                return t.reshape(t.shape[:-1] + (N_HEADS, D_HEAD)).swapaxes(-2, -3)
            Q = split_heads(Xn @ Wq + bq)
            K = split_heads(Xn @ Wk + bk)
            V = split_heads(Xn @ Wv + bv)
            scores = jnp.einsum('bhqd,bhkd->bhqk', Q, K) / jnp.sqrt(jnp.float32(D_HEAD))
            causal = jnp.tril(jnp.ones((n_ctx, n_ctx), dtype=bool))
            scores = jnp.where(causal, scores, jnp.float32(-jnp.inf))
            A = jax.nn.softmax(scores, axis=-1)
            AV = jnp.einsum('bhqk,bhkd->bhqd', A, V)
            AV = AV.swapaxes(-2, -3).reshape(X.shape[:-1] + (D_MODEL,))
            return AV @ Wo + bo
        return _mhsa(X, ln_g, ln_b, Wq, bq, Wk, bk, Wv, bv, Wo, bo)

    def _L0_xattn_ref(k, v, q, ssm_kernel, D, head_dim):
        import jax, jax.numpy as jnp
        import numpy as np
        B, HD, L = k.shape
        H = HD // head_dim
        fft_size = 2 * L
        k_ = k.reshape(B, H, head_dim, L)
        v_ = v.reshape(B, H, head_dim, L)
        q_ = q.reshape(B, H, head_dim, L)
        kv = jnp.einsum('bhil,bhjl->bijhl', k_, v_)
        kv_f = jnp.fft.rfft(kv, n=fft_size)
        kernel_f = jnp.fft.rfft(ssm_kernel, n=fft_size)
        y = jnp.fft.irfft(kv_f * kernel_f, n=fft_size)[..., :L]
        out = y + kv * D[None, None, None, :, None]
        out = jnp.einsum('bijhl,bhil->bjhl', out, q_)
        out = jnp.transpose(out, (0, 2, 1, 3)).reshape(B, H * head_dim, L)
        return out.astype(k.dtype)

    def _L0_ffn_ref(hidden_states, W_q, keys, down_embed, up_embed, gate_w, up_w, down_w):
        import jax, jax.numpy as jnp
        import numpy as np
        HIDDEN = 256
        INTER = 1024
        RETRIEVAL = 128
        NUM_EXPERTS = 512
        NUM_KEYS = 64
        TOP_K = 8
        B, S = (4, 256)
        b, s, h = hidden_states.shape
        n = b * s
        queries = (hidden_states @ W_q).reshape(2, n, RETRIEVAL // 2)
        routing = jnp.einsum('tnd,tdk->tnk', queries, keys)
        scores2, idx2 = jax.lax.top_k(routing, TOP_K)
        sx, sy = (scores2[0], scores2[1])
        ix, iy = (idx2[0], idx2[1])
        all_scores = (sx[:, :, None] + sy[:, None, :]).reshape(n, TOP_K * TOP_K)
        all_idx = (ix[:, :, None] * NUM_KEYS + iy[:, None, :]).reshape(n, TOP_K * TOP_K)
        scores, pk = jax.lax.top_k(all_scores, TOP_K)
        indices = jnp.take_along_axis(all_idx, pk, axis=-1)
        de = down_embed[indices]
        ue = up_embed[indices]
        x = hidden_states.reshape(n, h)
        ew = jnp.einsum('nh,nkh->nk', x, de)
        ew = jax.nn.silu(ew) * jax.nn.softmax(scores, axis=-1)
        experts_states = jnp.einsum('nk,nkh->nh', ew, ue).reshape(b, s, h)
        mlp = jax.nn.silu(x @ gate_w) * (x @ up_w) @ down_w
        return mlp.reshape(b, s, h) + experts_states
    x = _layernorm(x + _L0_attn_ref(x, L0_attn_ln_g, L0_attn_ln_b, L0_attn_Wq, L0_attn_bq, L0_attn_Wk, L0_attn_bk, L0_attn_Wv, L0_attn_bv, L0_attn_Wo, L0_attn_bo), axis=-1)
    x = _layernorm(x + _L0_xattn_ref(ctx_2048, ctx_2048, x, L0_xattn_ssm_kernel, L0_xattn_D, 8), axis=-1)
    x = _layernorm(x + _L0_ffn_ref(x, L0_ffn_W_q, L0_ffn_keys, L0_ffn_down_embed, L0_ffn_up_embed, L0_ffn_gate_w, L0_ffn_up_w, L0_ffn_down_w), axis=-1)
    return x

_drawn_inputs = setup_inputs


def setup_inputs(seed=0):
    import zlib

    import numpy as np

    out = dict(_drawn_inputs(seed))
    spreads = {'L0_attn_ln_g': (1.0, 0.6), 'L0_attn_ln_b': (0.0, 0.1)}
    factors = {'L0_attn_bq': 8.0,
     'L0_attn_bk': 8.0,
     'L0_ffn_W_q': 8.0,
     'L0_ffn_keys': 8.0,
     'L0_ffn_down_embed': 8.0,
     'L0_ffn_up_embed': 8.0}
    for name, (base, spread) in spreads.items():
        noise = np.random.default_rng([zlib.crc32(name.encode()), seed]).standard_normal(out[name].shape)
        drawn = base * np.exp(spread * noise) if base else spread * noise
        out[name] = jnp.asarray(drawn.astype(out[name].dtype))
    for name, factor in factors.items():
        out[name] = (out[name] * factor).astype(out[name].dtype)
    return out
```

```python
import concourse.bass as bass
from concourse import mybir
from contextlib import ExitStack

import numpy as np


def decoder_layer(nc, x, ctx_in, ln_g, ln_b, wq, bq, wk, bk, wv, bv, wo, bo, taps, skip, w_query, keys,
                  down_embed, up_embed, gate_w, up_w, down_w, out):
    fp32 = mybir.dt.float32
    bf16 = mybir.dt.bfloat16
    i32 = mybir.dt.int32
    u32 = mybir.dt.uint32
    ALU = mybir.AluOpType
    ACT = mybir.ActivationFunctionType
    AX = mybir.AxisListType

    P = 128
    B, S, D = x.shape
    KC = D // P
    H = 16
    DH = D // H
    HD = S // H
    HALF = H // KC
    RG = 4
    EPS = 1e-5
    MASKED = -1e30
    ND = HD // 2 + 1
    WR = ND - 2
    YW = HD + WR
    KW = HD + ND - 1
    NPR = ND * HD
    F = gate_w.shape[1]
    FM = F // P
    NE = down_embed.shape[0]
    EC = NE // P
    NK = keys.shape[2]
    TK = 8
    NT = B
    G = 2
    TG = NT // G
    LOWEST = -3.0e38

    es = ExitStack()
    with es:
        def sb(name, shape, dt=fp32):
            return es.enter_context(nc.sbuf_tensor(name, shape, dt))

        def sem(name):
            return es.enter_context(nc.semaphore(name))

        def over(ap, at, shape, dt=fp32):
            step = [1]
            for m in reversed(shape[2:]):
                step.insert(0, step[0] * m)
            v = bass.AP(ap.tensor, ap.offset + at, [list(ap.ap[0])] + [[a, m] for a, m in zip(step, shape[1:])])
            assert at + step[0] * shape[1] <= int(np.prod(ap.shape[1:]))
            return v if dt == fp32 else v.bitcast(dt)

        x_sb = sb("x_sb", [P, B, D])
        xb_sb = sb("xb_sb", [P, B, D])
        c_sb = sb("c_sb", [P, B, D])
        w_sb = {n: sb(f"w_{n}", [P, KC, D]) for n in ("q", "k", "v", "o")}
        g_col = sb("g_col", [P, KC])
        b_col = sb("b_col", [P, KC])
        bq_col = sb("bq_col", [P, KC])
        bk_col = sb("bk_col", [P, KC])
        bv_row = sb("bv_row", [P, D])
        bo_row = sb("bo_row", [P, D])
        skip_row = sb("skip_row", [P, H])
        toep = sb("toep", [P, H, D])
        wqr_sb = sb("wqr_sb", [P, KC, P])
        key_sb = sb("key_sb", [P, 2, NK])
        gate_sb = sb("gate_sb", [P, KC, F])
        up_sb = sb("up_sb", [P, KC, F])
        down_sb = sb("down_sb", [P, FM, D])
        de_sb = sb("de_sb", [P, EC, D])
        deT = sb("deT", [P, KC, NE])
        ue_sb = sb("ue_sb", [P, EC, D])
        ident = sb("ident", [P, P])
        anti = sb("anti", [P, P])
        ident_bf = sb("ident_bf", [P, P], bf16)
        ones_bf = sb("ones_bf", [P, P], bf16)
        mask_qk = sb("mask_qk", [P, P], bf16)
        mask_kq = sb("mask_kq", [P, P], bf16)
        zeros_bf = sb("zeros_bf", [P, P], bf16)
        head_sel = sb("head_sel", [P, 2])
        power = sb("power", [P, B])
        iota_i = sb("iota_i", [P, NK], i32)
        iota_f = sb("iota_f", [P, NK])
        weight_i = sb("weight_i", [P, TK], i32)
        weight_f = sb("weight_f", [P, TK])

        stat1 = sb("stat1", [P, B, 6])
        mv1 = sb("mv1", [P, B, 2])
        var1 = sb("var1", [P, B])
        rstd1 = sb("rstd1", [P, B])
        xh = sb("xh", [P, 2, D])
        xnT = sb("xnT", [P, 2, KC, P])
        qT = sb("qT", [P, 2, KC, 2, P])
        kT = sb("kT", [P, 2, KC, P])
        vext = sb("vext", [P, 2, H, DH + 1])
        negmax = sb("negmax", [P, RG, KC, 2], bf16)
        shift = sb("shift", [P, RG, KC * 2, P], bf16)
        shift32 = shift[:, :, :, :].rearrange("p r h q -> p (r h q)").bitcast(fp32)
        pT = sb("pT", [P, RG, KC, 2, P])
        rsum = sb("rsum", [P, H])
        av = sb("av", [P, D])
        avT = sb("avT", [P, KC, P])
        res = sb("res", [P, D])
        stat2 = sb("stat2", [P, 6])
        mv2 = sb("mv2", [P, 2])
        var2 = sb("var2", [P, 1])
        rstd2 = sb("rstd2", [P, 1])
        x1 = sb("x1", [P, B, D])

        kk = sb("kk", [P, KC, H, B, KW])
        kv = sb("kv", [P, 2, KC, 2, B, ND, HD])
        Y = sb("Y", [P, KC, H, B, ND, YW])
        QW = WR + HD + ND - 1
        qq = over(toep[:, :, :], 0, [P, 2, KC, H, QW])
        z = [over(pT[:, :, :, :, :], 0, [P, KC, TK, H, HD]),
             over(kv[:, :, :, :, :, :, :], 0, [P, KC, TK, H, HD])]
        res2 = over(shift32, 0, [P, 2, D])
        stat3 = sb("stat3", [P, 6])
        mv3 = sb("mv3", [P, 2])
        var3 = sb("var3", [P, 1])
        rstd3 = sb("rstd3", [P, 1])
        x2 = xb_sb
        x2T = over(c_sb[:, :, :], 0, [P, KC, B, P])
        qm = over(x_sb[:, :, :], 0, [P, 2 * B * P])

        rt = over(kk[:, :, :, :, :], 0, [P, NT, 2, NK])
        v8 = sb("v8", [P, NT, 2, TK])
        i8 = sb("i8", [P, NT, 2, TK], u32)
        f8 = sb("f8", [P, NT, 2, TK])
        fx64 = sb("fx64", [P, NT, TK])
        pair = over(kk[:, :, :, :, :], 1024, [P, NT, TK, TK])
        m8 = sb("m8", [P, NT, TK])
        pair_r = over(kk[:, :, :, :, :], 1536, [P, NT, TK, TK])
        sel = over(kk[:, :, :, :, :], 2048, [P, NT, TK, TK])
        ew = over(Y[:, :, :, :, :, :], 8192, [P, NT, TK, TK])
        tmp = over(kk[:, :, :, :, :], 2560, [P, NT, TK, TK])
        zs = sb("zs", [P, NT])
        rz = sb("rz", [P, NT])
        p511 = sb("p511", [P, NT])
        cnt = sb("cnt", [P, NT, TK])
        cx = sb("cx", [P, NT, TK])
        rank = over(Y[:, :, :, :, :, :], 8704, [P, NT, NK])
        ex = sb("ex", [P, NT, TK])
        ey = over(Y[:, :, :, :, :, :], 9216, [P, NT, NK])
        hT = Y[:, :, :, :, :, :].rearrange("p a b c d e -> p (a b c d e)")[:, 0:FM * B * P].rearrange(
            "p (m t) -> p m t", m=FM)
        pd = toep[:, :, :].rearrange("p h l -> p (h l)").rearrange("p (t a b) -> p t a b", t=NT, a=TK)
        gs = over(Y[:, :, :, :, :, :], 9728, [P, 2, 512])
        es_t = over(Y[:, :, :, :, :, :], 10752, [P, 2, NE])
        cT = over(Y[:, :, :, :, :, :], 11776, [P, 2, EC, P])
        res4 = over(Y[:, :, :, :, :, :], 12800, [P, 2, D])
        stat4 = sb("stat4", [P, 6])
        mv4 = sb("mv4", [P, 2])
        var4 = sb("var4", [P, 1])
        rstd4 = sb("rstd4", [P, 1])
        y_out = over(Y[:, :, :, :, :, :], 13312, [P, 2, D])

        ps = es.enter_context(nc.psum_tensor("ps", [P, 8, 512], fp32))
        sc_ps = ps[:, 0:RG, :]
        xT_ps = ps[:, 4, 0:D].rearrange("p (c t) -> p c t", c=KC)
        K_ps = xT_ps
        Q_ps = ps[:, 5, 0:D].rearrange("p (c t) -> p c t", c=KC)
        V_ps = ps[:, 5, D:2 * D]
        PV_ps = ps[:, 6, 0:H * (DH + 1)].rearrange("p (h e) -> p h e", h=H)
        avT_ps = ps[:, 6, 0:D].rearrange("p (c t) -> p c t", c=KC)
        wo_ps = ps[:, 6, 0:D]
        CW = B * NPR
        conv_ps = ps[:, 7, 0:CW]

        names = """crev_r l_x0 l_x1 l_g l_b l_bq l_bk l_bv l_bo l_skip l_toep l_ctx l_wq l_wk l_wv l_wo l_wqr l_key l_gate
        l_up l_down l_de l_ue consts id_r pool_o dve_o ones xb mv1_r var1_r rstd1_r ctxT kk_r toep_r kv_r conv_mm conv_ev y_r
        xh_r xT_r xnT_r kp_r qp0_r v_r q_r k_r vv_r sc_r max_r shift_r st_r p_r pv_r av_r avT_r avTs_r wo_r res_r var2_r
        rstd2_r x1_r x1T_r qq_r z_r red_r var3_r rstd3_r x2_r x2T_r x2Ts_r qp_r qm_r rt_r rts_r gu_r gs_r h_r
        ein_r ex_r pd_r ed_r es_r c_r cT_r cTs_r o_r var4_r rstd4_r yo_r stored act_o deT_ps deT_r qm0""".split()
        s = {n: sem(n) for n in names}

        def view(ap, dims, off=0):
            return bass.AP(ap.tensor, ap.offset + off, [list(ap.ap[0])] + dims)

        def bc(ap, axis, n):
            a = ap.unsqueeze(axis)
            shape = list(a.shape)
            shape[axis] = n
            return a.to_broadcast(shape)

        blk = es.enter_context(nc.Block())

        @blk.sync
        def _(sp):
            xr = x.rearrange("b t d -> t b d")
            sp.dma_start(x_sb[:, 0:1, :], xr[:, 0:1, :]).then_inc(s["l_x0"], 16)
            sp.dma_start(x_sb[:, 1:B, :], xr[:, 1:B, :]).then_inc(s["l_x1"], 16)
            sp.dma_start(c_sb[:, :, :], ctx_in.rearrange("b t d -> t b d")).then_inc(s["l_ctx"], 16)
            for n, w in (("q", wq), ("k", wk), ("v", wv)):
                sp.dma_start(w_sb[n][:, :, :], w.rearrange("(c p) n -> p c n", p=P)).then_inc(s[f"l_w{n}"], 16)
            W = taps.shape[1]
            sp.dma_start(toep[:, :, :], bass.AP(taps.tensor, taps.offset, [[1, P], [W, H], [1, D]])
                         ).then_inc(s["l_toep"], 16)
            sp.dma_start(w_sb["o"][:, :, :], wo.rearrange("(c p) n -> p c n", p=P)).then_inc(s["l_wo"], 16)
            sp.dma_start(de_sb[:, :, :], down_embed.rearrange("(c p) n -> p c n", p=P)).then_inc(s["l_de"], 16)
            sp.dma_start(gate_sb[:, :, :], gate_w.rearrange("(c p) n -> p c n", p=P)).then_inc(s["l_gate"], 16)
            sp.dma_start(up_sb[:, :, :], up_w.rearrange("(c p) n -> p c n", p=P)).then_inc(s["l_up"], 16)
            sp.dma_start(down_sb[:, :, :], down_w.rearrange("(c p) n -> p c n", p=P)).then_inc(s["l_down"], 16)
            sp.dma_start(ue_sb[:, :, :], up_embed.rearrange("(c p) n -> p c n", p=P)).then_inc(s["l_ue"], 16)
            for t in range(NT):
                sp.wait_ge(s["yo_r"], t + 1)
                sp.dma_start(out[t, :, :], y_out[:, t % 2, :]).then_inc(s["stored"], 16)
                sp.wait_ge(s["stored"], 16 * (t + 1))

        @blk.gpsimd
        def _(pool):
            n = [0]

            def link(ins):
                n[0] += 1
                ins.then_inc(s["pool_o"], 1)
                pool.wait_ge(s["pool_o"], n[0])

            link(nc.gpsimd.memset(ident[:, :], 0.0))
            nc.gpsimd.affine_select(out=ident[:, :], in_=ident[:, :], compare_op=ALU.not_equal, fill=1.0, base=0,
                                    pattern=[[-1, P]], channel_multiplier=1).then_inc(s["id_r"], 1)
            link(nc.gpsimd.memset(anti[:, :], 0.0))
            nc.gpsimd.affine_select(out=anti[:, :], in_=anti[:, :], compare_op=ALU.not_equal, fill=1.0, base=1 - P,
                                    pattern=[[1, P]], channel_multiplier=1).then_inc(s["id_r"], 1)
            link(nc.gpsimd.memset(power[:, :], -0.5))
            nc.gpsimd.memset(ones_bf[:, :], 1.0).then_inc(s["consts"], 1)
            pool.wait_ge(s["var1_r"], 1)
            nc.gpsimd.tensor_tensor(rstd1[:, 0:1], var1[:, 0:1], power[:, 0:1], ALU.pow).then_inc(s["rstd1_r"], 1)
            link(nc.gpsimd.memset(zeros_bf[:, :], 0.0))
            nc.gpsimd.affine_select(out=mask_qk[:, :], in_=zeros_bf[:, :], compare_op=ALU.is_ge, fill=MASKED,
                                    base=0, pattern=[[-1, P]], channel_multiplier=1).then_inc(s["consts"], 1)
            nc.gpsimd.affine_select(out=mask_kq[:, :], in_=zeros_bf[:, :], compare_op=ALU.is_ge, fill=MASKED,
                                    base=0, pattern=[[1, P]], channel_multiplier=-1).then_inc(s["consts"], 1)
            pool.wait_ge(s["id_r"], 1)
            nc.gpsimd.tensor_copy(ident_bf[:, :], ident[:, :]).then_inc(s["consts"], 1)
            pool.wait_ge(s["var1_r"], 2)
            nc.gpsimd.tensor_tensor(rstd1[:, 1:B], var1[:, 1:B], power[:, 1:B], ALU.pow).then_inc(s["rstd1_r"], 1)
            nc.gpsimd.memset(vext[:, :, :, DH:DH + 1], 1.0).then_inc(s["ones"], 1)
            pool.wait_ge(s["kk_r"], B)
            kkw = kk[:, :, :, :, :].rearrange("p c h b i -> p (c h b) i")
            nc.gpsimd.tensor_copy(kkw[:, :, HD:KW], kkw[:, :, 0:KW - HD]).then_inc(s["kk_r"], 1)
            pool.wait_ge(s["l_bo"], 16)
            nc.gpsimd.tensor_tensor(xb_sb[:, :, :], x_sb[:, :, :], bc(bo_row[:, :], 1, B), ALU.add
                                    ).then_inc(s["xb"], 1)
            nc.gpsimd.iota(iota_i[:, :], pattern=[[1, NK]], base=0, channel_multiplier=0).then_inc(s["pool_o"], 1)
            nc.gpsimd.iota(weight_i[:, :], pattern=[[-1, TK]], base=TK, channel_multiplier=0).then_inc(s["pool_o"], 1)
            n[0] += 2
            pool.wait_ge(s["pool_o"], n[0])
            nc.gpsimd.tensor_copy(iota_f[:, :], iota_i[:, :]).then_inc(s["consts"], 1)
            nc.gpsimd.tensor_copy(weight_f[:, :], weight_i[:, :]).then_inc(s["consts"], 1)

            def attn_rstd(b):
                pool.wait_ge(s["var2_r"], b + 1)
                nc.gpsimd.tensor_tensor(rstd2[:, :], var2[:, :], power[:, 0:1], ALU.pow).then_inc(s["rstd2_r"], 1)

            for b in range(B):
                for r in range(RG):
                    pool.wait_ge(s["max_r"], RG * b + r + 1)
                    if b >= 1:
                        pool.wait_ge(s["st_r"], 2 * (b - 1) + r // 2 + 1)
                    nc.gpsimd.tensor_tensor(shift[:, r, :, :], bc(ident_bf[:, :], 1, KC * 2),
                                            bc(negmax[:, r, :, :].rearrange("p t e -> p (t e)"), 2, P), ALU.mult
                                            ).then_inc(s["shift_r"], 1)
                if b >= 1:
                    attn_rstd(b - 1)
                pool.wait_ge(s["conv_ev"], 2 * KC * (b + 1))
                for c in range(KC):
                    yv = Y[:, c, 2 * b:2 * b + 2, :, 1:1 + WR, :].rearrange("p h b d i -> p (h b) d i")
                    nc.gpsimd.tensor_copy(yv[:, :, :, 0:WR], yv[:, :, :, HD:YW]).then_inc(s["y_r"], 1)
            pool.wait_ge(s["xh_r"], B)
            nc.gpsimd.memset(qm, 0.0).then_inc(s["qm0"], 1)
            attn_rstd(B - 1)
            for b in range(B):
                pool.wait_ge(s["var3_r"], b + 1)
                nc.gpsimd.tensor_tensor(rstd3[:, :], var3[:, :], power[:, 0:1], ALU.pow).then_inc(s["rstd3_r"], 1)
            for t in range(NT):
                pool.wait_ge(s["var4_r"], t + 1)
                nc.gpsimd.tensor_tensor(rstd4[:, :], var4[:, :], power[:, 0:1], ALU.pow).then_inc(s["rstd4_r"], 1)

        def x2_cols(act, b):
            act.wait_ge(s["x2T_r"], b + 1)
            nc.scalar.copy(x2T[:, :, b, :], ps[:, 6, 0:D].rearrange("p (c t) -> p c t", c=KC)
                           ).then_inc(s["x2Ts_r"], 1)
            act.wait_ge(s["qp_r"], b + 1)
            if b == 0:
                act.wait_ge(s["qm0"], 1)
            cols = qm[:, 2 * P * b:2 * P * (b + 1)].rearrange("p (t e) -> p t e", e=2)
            for e in range(2):
                nc.scalar.copy(cols[64 * e:64 * e + 64, :, e], ps[64 * e:64 * e + 64, 7, 0:P]
                               ).then_inc(s["qm_r"], 1)

        @blk.scalar
        def _(act):
            for n, t, src in (("g", g_col, ln_g), ("b", b_col, ln_b), ("bq", bq_col, bq), ("bk", bk_col, bk)):
                act.dma_start(t[:, :], src.rearrange("(c p) -> p c", p=P),
                              allow_slow_non_contiguous=True).then_inc(s[f"l_{n}"], 16)
            act.dma_start(bv_row[:, :], bv.partition_broadcast(P)).then_inc(s["l_bv"], 16)
            act.dma_start(skip_row[:, :], skip.partition_broadcast(P)).then_inc(s["l_skip"], 16)
            act.dma_start(bo_row[:, :], bo.partition_broadcast(P)).then_inc(s["l_bo"], 16)
            act.dma_start(wqr_sb[:, :, :], w_query.rearrange("(c p) n -> p c n", p=P)).then_inc(s["l_wqr"], 16)
            for e in range(2):
                act.dma_start(key_sb[64 * e:64 * e + 64, :, :], keys.rearrange("t d k -> d t k")
                              ).then_inc(s["l_key"], 16)

            act.wait_ge(s["l_ctx"], 16)
            nc.scalar.copy(x1[:, :, :], view(c_sb[:, :, :], [[D, B], [-1, D]], D - 1)).then_inc(s["crev_r"], 1)
            for b in range(B):
                act.wait_ge(s["ctxT"], b + 1)
                nc.scalar.copy(kk[:, :, :, b, 0:HD], ps[:, b % 4, 0:D].rearrange("p (c h i) -> p c h i", c=KC, h=H)
                               ).then_inc(s["kk_r"], 1)

            def norm_cols(b):
                act.wait_ge(s["xT_r"], b + 1)
                if b == 0:
                    act.wait_ge(s["l_g"], 16)
                    act.wait_ge(s["l_b"], 16)
                if b >= 2:
                    act.wait_ge(s["v_r"], b - 1)
                for c in range(KC):
                    nc.scalar.activation(xnT[:, b % 2, c, :], xT_ps[:, c, :], ACT.Identity, bias=b_col[:, c:c + 1],
                                         scale=g_col[:, c:c + 1]).then_inc(s["xnT_r"], 1)

            def k_cols(b):
                act.wait_ge(s["kp_r"], b + 1)
                if b == 0:
                    act.wait_ge(s["l_bk"], 16)
                if b >= 2:
                    act.wait_ge(s["st_r"], 2 * (b - 1))
                for c in range(KC):
                    nc.scalar.activation(kT[:, b % 2, c, :], K_ps[:, c, :], ACT.Identity, bias=bk_col[:, c:c + 1]
                                         ).then_inc(s["k_r"], 1)

            def probs(b, r):
                act.wait_ge(s["st_r"], 2 * b + r // 2 + 1)
                if b >= 1:
                    act.wait_ge(s["pv_r"], 2 * (b - 1) + r // 2 + 1)
                nc.scalar.activation(pT[:, r, :, :, :].rearrange("p t e q -> p (t e q)"), sc_ps[:, r, :], ACT.Exp
                                     ).then_inc(s["p_r"], 1)

            def conv_out(h, c):
                act.wait_ge(s["conv_mm"], KC * h + c + 1)
                nc.scalar.copy(Y[:, c, h, :, :, WR:YW].rearrange("p b d i -> p (b d) i"),
                               conv_ps.rearrange("p (b i) -> p b i", i=HD)).then_inc(s["conv_ev"], 1)

            norm_cols(0)
            k_cols(0)
            for b in range(B):
                if b >= 1:
                    act.wait_ge(s["avT_r"], b)
                    nc.scalar.copy(avT[:, :, :], avT_ps).then_inc(s["avTs_r"], 1)
                conv_out(2 * b, 0)
                if b + 1 < B:
                    norm_cols(b + 1)
                conv_out(2 * b, 1)
                probs(b, 0)
                probs(b, 1)
                if b + 1 < B:
                    k_cols(b + 1)
                conv_out(2 * b + 1, 0)
                probs(b, 2)
                probs(b, 3)
                conv_out(2 * b + 1, 1)
            act.wait_ge(s["avT_r"], B)
            nc.scalar.copy(avT[:, :, :], avT_ps).then_inc(s["avTs_r"], 1)

            act.wait_ge(s["deT_ps"], 1)
            for c in range(KC):
                nc.scalar.copy(deT[:, c, :], ps[:, c, :]).then_inc(s["deT_r"], 1)

            for b in range(B):
                act.wait_ge(s["x1T_r"], b + 1)
                if b >= 2:
                    act.wait_ge(s["z_r"], 2 * KC * (b - 1))
                src = ps[:, 2 + b % 2, 0:D].rearrange("p (c h i) -> p (c h) i", c=KC, h=H)
                dst = qq[:, b % 2, :, :, :].rearrange("p c h i -> p (c h) i")
                nc.scalar.copy(dst[:, :, WR:WR + HD], src).then_inc(s["qq_r"], 1)
                nc.scalar.copy(dst[:, :, WR + HD:QW], src[:, :, 0:ND - 1]).then_inc(s["qq_r"], 1)
                nc.scalar.copy(dst[:, :, 0:WR], src[:, :, HD - WR:HD]).then_inc(s["qq_r"], 1)
                if b >= 1:
                    x2_cols(act, b - 1)
            x2_cols(act, B - 1)

            act.wait_ge(s["rt_r"], 1)
            for i in range(2):
                nc.scalar.copy(rt[:, 4 * i:4 * i + 4, :, :].rearrange("p t a k -> p (t a k)"), ps[:, i, :]
                               ).then_inc(s["rts_r"], 1)
            for u in range(G * FM):
                act.wait_ge(s["gu_r"], u + 1)
                if u >= 2:
                    act.wait_ge(s["h_r"], u - 1)
                nc.scalar.activation(gs[:, u % 2, :], ps[:, 2 + 2 * (u % 3), :], ACT.Silu).then_inc(s["gs_r"], 1)
                if u == 10:
                    act.wait_ge(s["ein_r"], 3)
                    nc.scalar.activation(ew[:, :, :, :].rearrange("p t a b -> p (t a b)"),
                                         ew[:, :, :, :].rearrange("p t a b -> p (t a b)"), ACT.Exp
                                         ).then_inc(s["ex_r"], 1)
                    nc.scalar.activation(ex[:, :, :], ex[:, :, :], ACT.Exp).then_inc(s["ex_r"], 1)
                    nc.scalar.activation(ey[:, :, :], ey[:, :, :], ACT.Exp).then_inc(s["ex_r"], 1)

            def gate_expert(t):
                act.wait_ge(s["ed_r"], t + 1)
                if t >= 2:
                    act.wait_ge(s["cT_r"], t - 1)
                nc.scalar.activation(es_t[:, t % 2, :], ps[:, 6 + t % 2, :], ACT.Silu).then_inc(s["es_r"], 1)

            gate_expert(0)
            for t in range(NT):
                if t + 1 < NT:
                    gate_expert(t + 1)
                act.wait_ge(s["cT_r"], t + 1)
                if t >= 2:
                    act.wait_ge(s["o_r"], t - 1)
                nc.scalar.copy(cT[:, t % 2, :, :].rearrange("p c t -> p (c t)"), ps[:, 4 + t % 2, :]
                               ).then_inc(s["cTs_r"], 1)

        @blk.vector
        def _(dve):
            n = [0]

            def link(ins):
                n[0] += 1
                ins.then_inc(s["dve_o"], 1)
                dve.wait_ge(s["dve_o"], n[0])

            V = nc.vector

            def stats1(b):
                link(V.bn_stats(stat1[:, b, :], x_sb[:, b, :]))
                V.bn_aggr(mv1[:, b, :], stat1[:, b, :]).then_inc(s["mv1_r"], 1)

            def xhat(b):
                if b >= 2:
                    dve.wait_ge(s["xT_r"], b - 1)
                V.tensor_scalar(xh[:, b % 2, :], x_sb[:, b, :], mv1[:, b, 0:1], rstd1[:, b:b + 1], ALU.subtract,
                                ALU.mult).then_inc(s["xh_r"], 1)

            def kv_products(b):
                if b >= 2:
                    dve.wait_ge(s["conv_mm"], 2 * KC * (b - 1))
                for c in range(KC):
                    src = kk[:, c, 2 * b:2 * b + 2, :, 0:HD]
                    V.tensor_tensor(kv[:, b % 2, c, :, :, :, :].rearrange("p h b d i -> p (h b) d i"),
                                    view(src, [[KW, 2 * B], [0, ND], [1, HD]]),
                                    view(src, [[KW, 2 * B], [1, ND], [1, HD]]), ALU.mult).then_inc(s["kv_r"], 1)

            def q_cols(b):
                dve.wait_ge(s["v_r"], b + 1)
                if b >= 2:
                    dve.wait_ge(s["st_r"], 2 * (b - 1))
                for c in range(KC):
                    for e in range(2):
                        V.tensor_scalar(qT[:, b % 2, c, e, :], Q_ps[:, c, :], bq_col[:, c:c + 1],
                                        head_sel[:, e:e + 1], ALU.add, ALU.mult).then_inc(s["q_r"], 1)

            def v_rows(b):
                dve.wait_ge(s["v_r"], b + 1)
                if b >= 2:
                    dve.wait_ge(s["pv_r"], 2 * (b - 1))
                V.tensor_tensor(vext[:, b % 2, :, 0:DH], V_ps.rearrange("p (h e) -> p h e", h=H),
                                bv_row[:, :].rearrange("p (h e) -> p h e", h=H), ALU.add).then_inc(s["vv_r"], 1)

            def row_max(b, r):
                if r == 0:
                    dve.wait_ge(s["sc_r"], b + 1)
                if b >= 1:
                    dve.wait_ge(s["shift_r"], RG * (b - 1) + r + 1)
                V.tensor_reduce(negmax[:, r, :, :].rearrange("p t e -> p (t e)"),
                                sc_ps[:, r, :].rearrange("p (h k) -> p h k", k=P), AX.X, ALU.max, negate=True
                                ).then_inc(s["max_r"], 1)

            def attn_norm(b):
                dve.wait_ge(s["pv_r"], 2 * (b + 1))
                link(V.reciprocal(rsum[:, :], PV_ps[:, :, DH]))
                if b >= 1:
                    dve.wait_ge(s["avT_r"], b)
                V.tensor_tensor(av[:, :].rearrange("p (h e) -> p h e", h=H), PV_ps[:, :, 0:DH],
                                bc(rsum[:, :], 2, DH), ALU.mult).then_inc(s["av_r"], 1)

            def attn_res(b):
                dve.wait_ge(s["wo_r"], b + 1)
                if b == 0:
                    dve.wait_ge(s["xb"], 1)
                V.tensor_tensor(res[:, :], wo_ps, xb_sb[:, b, :], ALU.add).then_inc(s["res_r"], 1)
                dve.wait_ge(s["res_r"], b + 1)
                link(V.bn_stats(stat2[:, :], res[:, :]))
                link(V.bn_aggr(mv2[:, :], stat2[:, :]))
                V.tensor_scalar(var2[:, :], mv2[:, 1:2], EPS, None, ALU.add).then_inc(s["var2_r"], 1)

            def attn_out(b):
                dve.wait_ge(s["rstd2_r"], b + 1)
                V.tensor_scalar(x1[:, b, :], res[:, :], mv2[:, 0:1], rstd2[:, :], ALU.subtract, ALU.mult
                                ).then_inc(s["x1_r"], 1)

            dve.wait_ge(s["l_x0"], 16)
            stats1(0)
            dve.wait_ge(s["mv1_r"], 1)
            V.tensor_scalar(var1[:, 0:1], mv1[:, 0, 1:2], EPS, None, ALU.add).then_inc(s["var1_r"], 1)
            dve.wait_ge(s["id_r"], 1)
            for e in range(2):
                link(V.tensor_reduce(head_sel[:, e:e + 1],
                                     ident[:, :].rearrange("p (g e i) -> p g e i", g=RG, e=2)[:, :, e, :],
                                     AX.XY, ALU.add))
            link(V.tensor_scalar(head_sel[:, :], head_sel[:, :], float(DH) ** -0.5, None, ALU.mult))
            dve.wait_ge(s["rstd1_r"], 1)
            xhat(0)
            dve.wait_ge(s["l_x1"], 16)
            for b in range(1, B):
                stats1(b)
            dve.wait_ge(s["mv1_r"], B)
            V.tensor_scalar(var1[:, 1:B], mv1[:, 1:B, 1], EPS, None, ALU.add).then_inc(s["var1_r"], 1)
            dve.wait_ge(s["l_bq"], 16)
            q_cols(0)
            dve.wait_ge(s["l_bv"], 16)
            v_rows(0)
            dve.wait_ge(s["rstd1_r"], 2)
            xhat(1)
            dve.wait_ge(s["l_toep"], 16)
            dve.wait_ge(s["l_skip"], 16)
            dve.wait_ge(s["id_r"], 2)
            dtmp = Y[:, 0, :, :, :, :].rearrange("p h b d i -> p (h b d i)")[:, 0:H * P].rearrange(
                "p (h l) -> p h l", h=H)
            link(V.tensor_tensor(dtmp, bc(anti[:, :], 1, H), bc(skip_row[:, :], 2, P), ALU.mult))
            V.tensor_tensor(toep[:, :, 0:P], toep[:, :, 0:P], dtmp, ALU.add).then_inc(s["toep_r"], 1)
            dve.wait_ge(s["toep_r"], 1)
            dve.wait_ge(s["kk_r"], B + 1)
            kv_products(0)

            for b in range(B):
                if b >= 1:
                    attn_norm(b - 1)
                for r in range(RG):
                    row_max(b, r)
                if b + 1 < B:
                    kv_products(b + 1)
                if b >= 1:
                    attn_res(b - 1)
                if b + 1 < B:
                    q_cols(b + 1)
                    v_rows(b + 1)
                if b >= 1:
                    attn_out(b - 1)
                if b + 2 < B:
                    xhat(b + 2)
            attn_norm(B - 1)
            attn_res(B - 1)
            attn_out(B - 1)

            def cross_products(b):
                dve.wait_ge(s["qq_r"], 3 * (b + 1))
                if b == 0:
                    dve.wait_ge(s["y_r"], KC * B)
                if b >= 2:
                    dve.wait_ge(s["red_r"], b - 1)
                row = B * ND * YW
                for c in range(KC):
                    yb = Y[:, c, :, b, :, :]
                    q0 = qq[:, b % 2, c, :, :]
                    V.tensor_tensor(z[b % 2][:, c, 0:ND, :, :], view(yb, [[YW, ND], [row, H], [1, HD]], WR),
                                    view(q0, [[1, ND], [QW, H], [1, HD]], WR), ALU.mult).then_inc(s["z_r"], 1)
                    V.tensor_tensor(z[b % 2][:, c, ND:TK, :, :], view(yb, [[YW - 1, WR], [row, H], [1, HD]], YW + WR - 1),
                                    view(q0, [[-1, WR], [QW, H], [1, HD]], WR - 1), ALU.mult).then_inc(s["z_r"], 1)

            def cross_res(b):
                dve.wait_ge(s["red_r"], b + 1)
                r = res2[:, b % 2, :]
                link(V.tensor_tensor(r, ps[:, 4 + b % 2, 0:D], x1[:, b, :], ALU.add))
                link(V.bn_stats(stat3[:, :], r))
                link(V.bn_aggr(mv3[:, :], stat3[:, :]))
                V.tensor_scalar(var3[:, :], mv3[:, 1:2], EPS, None, ALU.add).then_inc(s["var3_r"], 1)
                dve.wait_ge(s["rstd3_r"], b + 1)
                V.tensor_scalar(x2[:, b, :], r, mv3[:, 0:1], rstd3[:, :], ALU.subtract, ALU.mult
                                ).then_inc(s["x2_r"], 1)

            for b in range(B):
                cross_products(b)
                if b >= 1:
                    cross_res(b - 1)
            cross_res(B - 1)

            def hidden(u):
                dve.wait_ge(s["gs_r"], u + 1)
                g, m = divmod(u, FM)
                V.tensor_tensor(hT[:, m, 512 * g:512 * (g + 1)], ps[:, 3 + 2 * (u % 3), :], gs[:, u % 2, :], ALU.mult
                                ).then_inc(s["h_r"], 1)

            dve.wait_ge(s["rts_r"], 2)
            for u in range(NT):
                hidden(u)
                link(V.max(v8[:, u, 0, :], rt[:, u, 0, :]))
                link(V.max(v8[:, u, 1, :], rt[:, u, 1, :]))
                link(V.max_index(i8[:, u, 0, :], v8[:, u, 0, :], rt[:, u, 0, :]))
                link(V.max_index(i8[:, u, 1, :], v8[:, u, 1, :], rt[:, u, 1, :]))
            link(V.tensor_tensor(pair[:, :, :, :], bc(v8[:, :, 0, :], 3, TK), bc(v8[:, :, 1, :], 2, TK), ALU.add))
            link(V.tensor_copy(f8[:, :, :, :], i8[:, :, :, :]))
            hidden(8)
            for t in range(NT):
                pr = pair[:, t, :, :].rearrange("p a b -> p (a b)")
                link(V.max(m8[:, t, :], pr))
                link(V.match_replace(pair_r[:, t, :, :].rearrange("p a b -> p (a b)"), m8[:, t, :], pr, LOWEST))
            hidden(9)
            V.tensor_tensor(ew[:, :, :, :].rearrange("p t a b -> p t (a b)"),
                            pair[:, :, :, :].rearrange("p t a b -> p t (a b)"), bc(m8[:, :, 0], 2, TK * TK),
                            ALU.subtract).then_inc(s["ein_r"], 1)
            V.tensor_tensor(ex[:, :, :], rt[:, :, 0, 0:TK], bc(v8[:, :, 0, 0], 2, TK), ALU.subtract
                            ).then_inc(s["ein_r"], 1)
            V.tensor_tensor(ey[:, :, :], rt[:, :, 1, :], bc(v8[:, :, 1, 0], 2, NK), ALU.subtract
                            ).then_inc(s["ein_r"], 1)
            link(V.tensor_tensor(sel[:, :, :, :], pair_r[:, :, :, :], pair[:, :, :, :], ALU.not_equal))
            link(V.tensor_reduce(cnt[:, :, :], sel[:, :, :, :], AX.X, ALU.add))
            hidden(10)
            link(V.tensor_tensor(tmp[:, :, :, :], bc(f8[:, :, 0, :], 2, TK),
                                 view(iota_f[:, 0:TK], [[0, NT], [1, TK], [0, TK]]), ALU.is_equal))
            link(V.tensor_tensor(tmp[:, :, :, :], tmp[:, :, :, :], bc(cnt[:, :, :], 2, TK), ALU.mult))
            link(V.tensor_reduce(cx[:, :, :], tmp[:, :, :, :], AX.X, ALU.add))
            hidden(11)
            big = pd.rearrange("p t a b -> p (t a b)").rearrange("p (t k b) -> p t k b", t=NT, k=NK)
            link(V.tensor_tensor(big, bc(f8[:, :, 1, :], 2, NK), view(iota_f[:, :], [[0, NT], [1, NK], [0, TK]]),
                                 ALU.is_equal))
            hidden(12)
            link(V.tensor_tensor(big, big, view(weight_f[:, :], [[0, NT], [0, NK], [1, TK]]), ALU.mult))
            hidden(13)
            link(V.tensor_reduce(rank[:, :, :], big, AX.X, ALU.add))
            hidden(14)
            dve.wait_ge(s["ex_r"], 3)
            link(V.tensor_tensor(ew[:, :, :, :], ew[:, :, :, :], sel[:, :, :, :], ALU.mult))
            link(V.tensor_reduce(zs[:, :], ew[:, :, :, :], AX.XY, ALU.add))
            link(V.reciprocal(rz[:, :], zs[:, :]))
            link(V.tensor_scalar(fx64[:, :, :], f8[:, :, 0, :], float(NK), None, ALU.mult))
            link(V.tensor_tensor(tmp[:, :, :, :], bc(fx64[:, :, :], 3, TK), bc(f8[:, :, 1, :], 2, TK), ALU.add))
            fl = "p t a b -> p (t a b)"
            link(V.scalar_tensor_tensor(tmp[:, :, :, :].rearrange(fl), tmp[:, :, :, :].rearrange(fl), float(NE - 1),
                                        ew[:, :, :, :].rearrange(fl), ALU.is_ge, ALU.mult))
            link(V.tensor_reduce(p511[:, :], tmp[:, :, :, :], AX.XY, ALU.add))
            link(V.tensor_tensor(p511[:, :], p511[:, :], rz[:, :], ALU.mult))
            link(V.tensor_tensor(ex[:, :, :], ex[:, :, :], bc(rz[:, :], 2, TK), ALU.mult))
            hidden(15)
            for t in range(NT):
                link(V.tensor_tensor(pd[:, t, :, :], bc(rank[:, t, :], 1, TK), bc(cx[:, t, :], 2, NK), ALU.add))
                link(V.scalar_tensor_tensor(pd[:, t, :, :], pd[:, t, :, :], TK + 0.5, bc(ey[:, t, :], 1, TK),
                                            ALU.is_gt, ALU.mult))
                link(V.tensor_tensor(pd[:, t, :, :], pd[:, t, :, :], bc(ex[:, t, :], 2, NK), ALU.mult))
                link(V.tensor_copy(pd[:, t, TK - 1, NK - 1:NK], p511[:, t:t + 1]))

            def last_norm(t):
                dve.wait_ge(s["o_r"], t + 1)
                r = res4[:, t % 2, :]
                link(V.tensor_tensor(r, ps[:, t % 2, 0:D], x2[:, t, :], ALU.add))
                link(V.bn_stats(stat4[:, :], r))
                link(V.bn_aggr(mv4[:, :], stat4[:, :]))
                V.tensor_scalar(var4[:, :], mv4[:, 1:2], EPS, None, ALU.add).then_inc(s["var4_r"], 1)
                dve.wait_ge(s["rstd4_r"], t + 1)
                if t >= 2:
                    dve.wait_ge(s["stored"], 16 * (t - 1))
                V.tensor_scalar(y_out[:, t % 2, :], r, mv4[:, 0:1], rstd4[:, :], ALU.subtract, ALU.mult
                                ).then_inc(s["yo_r"], 1)

            for t in range(NT):
                dve.wait_ge(s["es_r"], t + 1)
                V.tensor_tensor(es_t[:, t % 2, :], es_t[:, t % 2, :], pd[:, t, :, :].rearrange("p a b -> p (a b)"),
                                ALU.mult).then_inc(s["c_r"], 1)
                if t >= 1:
                    last_norm(t - 1)
            last_norm(NT - 1)

        @blk.tensor
        def _(pe):
            M = nc.tensor.matmul
            T = nc.tensor.transpose

            def x_transpose(b):
                pe.wait_ge(s["xh_r"], b + 1)
                if b >= 1:
                    pe.wait_ge(s["k_r"], KC * b)
                for c in range(KC):
                    last = T(xT_ps[:, c, :], xh[:, b % 2, c * P:(c + 1) * P], ident[:, :])
                last.then_inc(s["xT_r"], 1)

            def project(b):
                pe.wait_ge(s["xnT_r"], KC * (b + 1))
                if b == 0:
                    pe.wait_ge(s["l_wq"], 16)
                    pe.wait_ge(s["l_wk"], 16)
                    pe.wait_ge(s["l_wv"], 16)
                if b >= 1:
                    pe.wait_ge(s["q_r"], 2 * KC * b)
                    pe.wait_ge(s["vv_r"], b)
                for w, dst, done in (("k", K_ps, "kp_r"), ("q", Q_ps, "qp0_r")):
                    for c in range(KC):
                        for k in range(KC):
                            last = M(dst[:, c, :], w_sb[w][:, k, c * P:(c + 1) * P], xnT[:, b % 2, k, :],
                                     start=(k == 0), stop=(k == KC - 1))
                    last.then_inc(s[done], 1)
                for k in range(KC):
                    last = M(V_ps, xnT[:, b % 2, k, :], w_sb["v"][:, k, :], start=(k == 0), stop=(k == KC - 1))
                last.then_inc(s["v_r"], 1)

            def scores(b):
                pe.wait_ge(s["q_r"], 2 * KC * (b + 1))
                pe.wait_ge(s["k_r"], KC * (b + 1))
                if b >= 1:
                    pe.wait_ge(s["p_r"], RG * b)
                for r in range(RG):
                    M(sc_ps[:, r, :], ident_bf[:, :], bc(mask_qk[:, :], 1, 4), start=True,
                      stop=False)
                for t in range(KC):
                    for e in range(2):
                        for r in range(RG):
                            i = 2 * t + e
                            last = M(sc_ps[:, r, i * P:(i + 1) * P], qT[32 * r:32 * r + 32, b % 2, t, e, :],
                                     kT[32 * r:32 * r + 32, b % 2, t, :], start=False, stop=(i == 3))
                last.then_inc(s["sc_r"], 1)

            def scores_t(b, half):
                pe.wait_ge(s["shift_r"], RG * b + 2 * half + 2)
                rr = range(2 * half, 2 * half + 2)
                for r in rr:
                    M(sc_ps[:, r, :], ident_bf[:, :], bc(mask_kq[:, :], 1, 4), start=True,
                      stop=False)
                    M(sc_ps[:, r, :], ones_bf[:, :], shift[:, r, :, :].rearrange("p e q -> p (e q)"), start=False,
                      stop=False)
                for t in range(KC):
                    for r in rr:
                        last = M(sc_ps[:, r, 2 * t * P:2 * (t + 1) * P], kT[32 * r:32 * r + 32, b % 2, t, :],
                                 qT[32 * r:32 * r + 32, b % 2, t, :, :].rearrange("p e q -> p (e q)"), start=False,
                                 stop=(t == KC - 1))
                last.then_inc(s["st_r"], 1)

            def values(b, half):
                pe.wait_ge(s["p_r"], RG * b + 2 * half + 2)
                pe.wait_ge(s["vv_r"], b + 1)
                if b == 0:
                    pe.wait_ge(s["ones"], 1)
                if b >= 1:
                    pe.wait_ge(s["res_r"], b)
                for r in range(2 * half, 2 * half + 2):
                    for t in range(KC):
                        for e in range(2):
                            h = t * HALF + 2 * r + e
                            last = M(PV_ps[:, h, :], pT[:, r, t, e, :], vext[:, b % 2, h, :], start=True, stop=True)
                last.then_inc(s["pv_r"], 1)

            def out_project(b):
                pe.wait_ge(s["av_r"], b + 1)
                if b == 0:
                    pe.wait_ge(s["l_wo"], 16)
                for c in range(KC):
                    last = T(avT_ps[:, c, :], av[:, c * P:(c + 1) * P], ident[:, :])
                last.then_inc(s["avT_r"], 1)

            def out_project2(b):
                pe.wait_ge(s["avTs_r"], b + 1)
                for c in range(KC):
                    last = M(wo_ps, avT[:, c, :], w_sb["o"][:, c, :], start=(c == 0), stop=(c == KC - 1))
                last.then_inc(s["wo_r"], 1)

            def conv(h, c):
                pe.wait_ge(s["kv_r"], KC * (h // 2 + 1))
                if h == 0:
                    pe.wait_ge(s["toep_r"], 1)
                i = KC * h + c
                if i >= 1:
                    pe.wait_ge(s["conv_ev"], i)
                for k in range(c + 1):
                    d = c - k
                    last = M(conv_ps, toep[:, h, d * P:(d + 1) * P],
                             kv[:, h // 2 % 2, k, h % 2, :, :, :].rearrange("p b d i -> p (b d i)"), start=(k == 0),
                             stop=(k == c))
                last.then_inc(s["conv_mm"], 1)

            pe.wait_ge(s["id_r"], 1)
            x_transpose(0)
            pe.wait_ge(s["crev_r"], 1)
            for b in range(B):
                if b >= 4:
                    pe.wait_ge(s["kk_r"], b - 3)
                for c in range(KC):
                    last = T(ps[:, b % 4, c * P:(c + 1) * P], x1[:, b, (KC - 1 - c) * P:(KC - c) * P], ident[:, :])
                last.then_inc(s["ctxT"], 1)
            project(0)
            pe.wait_ge(s["kk_r"], B)
            pe.wait_ge(s["consts"], 4)
            for b in range(B):
                if b >= 1:
                    out_project(b - 1)
                scores(b)
                conv(2 * b, 0)
                if b + 1 < B:
                    x_transpose(b + 1)
                if b >= 1:
                    out_project2(b - 1)
                conv(2 * b, 1)
                scores_t(b, 0)
                if b + 1 < B:
                    project(b + 1)
                conv(2 * b + 1, 0)
                scores_t(b, 1)
                values(b, 0)
                conv(2 * b + 1, 1)
                values(b, 1)
            out_project(B - 1)
            out_project2(B - 1)

            pe.wait_ge(s["l_de"], 16)
            pe.wait_ge(s["p_r"], RG * B)
            for c in range(KC):
                for e in range(EC):
                    last = T(ps[:, c, e * P:(e + 1) * P], de_sb[:, e, c * P:(c + 1) * P], ident[:, :])
            last.then_inc(s["deT_ps"], 1)

            def cross_queries(b):
                pe.wait_ge(s["x1_r"], b + 1)
                if b >= 2:
                    pe.wait_ge(s["qq_r"], 3 * (b - 1))
                for c in range(KC):
                    last = T(ps[:, 2 + b % 2, c * P:(c + 1) * P], x1[:, b, c * P:(c + 1) * P], ident[:, :])
                last.then_inc(s["x1T_r"], 1)

            def cross_sum(b):
                pe.wait_ge(s["z_r"], 2 * KC * (b + 1))
                if b >= 2:
                    pe.wait_ge(s["x2_r"], b - 1)
                for c in range(KC):
                    for t in range(TK):
                        last = M(ps[:, 4 + b % 2, c * P:(c + 1) * P], z[b % 2][:, c, t, :, :].rearrange("p h j -> p (h j)"), ident[:, :],
                                 start=(t == 0), stop=(t == TK - 1))
                last.then_inc(s["red_r"], 1)

            def route_query(b):
                pe.wait_ge(s["x2_r"], b + 1)
                if b >= 1:
                    pe.wait_ge(s["x2Ts_r"], b)
                for c in range(KC):
                    last = T(ps[:, 6, c * P:(c + 1) * P], x2[:, b, c * P:(c + 1) * P], ident[:, :])
                last.then_inc(s["x2T_r"], 1)
                pe.wait_ge(s["x2Ts_r"], b + 1)
                if b >= 1:
                    pe.wait_ge(s["qm_r"], 2 * b)
                else:
                    pe.wait_ge(s["l_wqr"], 16)
                for c in range(KC):
                    last = M(ps[:, 7, 0:P], wqr_sb[:, c, :], x2T[:, c, b, :], start=(c == 0), stop=(c == KC - 1))
                last.then_inc(s["qp_r"], 1)

            cross_queries(0)
            for b in range(B):
                if b + 1 < B:
                    cross_queries(b + 1)
                cross_sum(b)
                if b >= 1:
                    route_query(b - 1)
            route_query(B - 1)

            pe.wait_ge(s["deT_r"], KC)
            pe.wait_ge(s["qm_r"], 2 * B)
            pe.wait_ge(s["l_key"], 32)
            for t in range(NT):
                for a in range(2):
                    c0 = (t % 4) * 2 * NK + a * NK
                    col = (a * NT + t) * P
                    last = M(ps[:, t // 4, c0:c0 + NK], qm[:, col:col + P], key_sb[:, a, :], start=True, stop=True)
            last.then_inc(s["rt_r"], 1)

            pe.wait_ge(s["l_gate"], 16)
            pe.wait_ge(s["l_up"], 16)
            for u in range(G * FM):
                g, m = divmod(u, FM)
                if u >= 3:
                    pe.wait_ge(s["h_r"], u - 2)
                for a, w in enumerate((gate_sb, up_sb)):
                    for k in range(KC):
                        last = M(ps[:, 2 + 2 * (u % 3) + a, :], w[:, k, m * P:(m + 1) * P],
                                 x2T[:, k, TG * g:TG * (g + 1), :].rearrange("p b t -> p (b t)"), start=(k == 0),
                                 stop=(k == KC - 1))
                last.then_inc(s["gu_r"], 1)

            def expert_in(t):
                if t >= 2:
                    pe.wait_ge(s["es_r"], t - 1)
                for k in range(KC):
                    last = M(ps[:, 6 + t % 2, :], x2T[:, k, t, :], deT[:, k, :], start=(k == 0), stop=(k == KC - 1))
                last.then_inc(s["ed_r"], 1)

            pe.wait_ge(s["h_r"], G * FM)
            pe.wait_ge(s["rts_r"], 2)
            pe.wait_ge(s["l_down"], 16)
            pe.wait_ge(s["l_ue"], 16)
            expert_in(0)
            for t in range(NT):
                if t + 1 < NT:
                    expert_in(t + 1)
                if t >= 2:
                    pe.wait_ge(s["yo_r"], t - 1)
                for m in range(FM):
                    M(ps[:, t % 2, 0:D], hT[:, m, t * P:(t + 1) * P], down_sb[:, m, :], start=(m == 0), stop=False)
                pe.wait_ge(s["c_r"], t + 1)
                if t >= 2:
                    pe.wait_ge(s["cTs_r"], t - 1)
                for e in range(EC):
                    last = T(ps[:, 4 + t % 2, e * P:(e + 1) * P], es_t[:, t % 2, e * P:(e + 1) * P], ident[:, :])
                last.then_inc(s["cT_r"], 1)
                pe.wait_ge(s["cTs_r"], t + 1)
                for e in range(EC):
                    last = M(ps[:, t % 2, 0:D], cT[:, t % 2, e, :], ue_sb[:, e, :], start=False, stop=(e == EC - 1))
                last.then_inc(s["o_r"], 1)


def kernel(**inputs):
    import numpy as np
    import concourse.bacc as bacc
    from concourse.bass_utils import run_bass_kernel_spmd

    names = ['x', 'ctx_2048', 'L0_attn_ln_g', 'L0_attn_ln_b', 'L0_attn_Wq', 'L0_attn_bq', 'L0_attn_Wk', 'L0_attn_bk',
             'L0_attn_Wv', 'L0_attn_bv', 'L0_attn_Wo', 'L0_attn_bo', 'L0_xattn_ssm_kernel', 'L0_xattn_D',
             'L0_ffn_W_q', 'L0_ffn_keys', 'L0_ffn_down_embed', 'L0_ffn_up_embed', 'L0_ffn_gate_w', 'L0_ffn_up_w',
             'L0_ffn_down_w']
    nc = bacc.Bacc("TRN2", target_bir_lowering=False, num_devices=1)
    arrays, args = {}, []
    for name in names:
        a = np.ascontiguousarray(inputs[name])
        if name == 'L0_xattn_ssm_kernel':
            padded = np.zeros((a.shape[0], 127 + a.shape[1]), a.dtype)
            padded[:, 127:] = a
            a = padded
        arrays[f"in_{name}"] = a
        args.append(nc.dram_tensor(f"in_{name}", a.shape, mybir.dt.from_np(a.dtype), kind="ExternalInput").ap())
    shape = tuple(inputs['x'].shape)
    args.append(nc.dram_tensor("out_0", shape, mybir.dt.float32, kind="ExternalOutput").ap())
    decoder_layer(nc, *args)
    r = run_bass_kernel_spmd(nc, [arrays], core_ids=[0])
    return r.results[0]["out_0"]
```

```python
import concourse.bass as bass
from concourse import mybir
from contextlib import ExitStack

import numpy as np


def decoder_layer(nc, x, ctx_in, ln_g, ln_b, wq, bq, wk, bk, wv, bv, wo, bo, taps, skip, w_query, keys,
                  down_embed, up_embed, gate_w, up_w, down_w, out):
    fp32 = mybir.dt.float32
    bf16 = mybir.dt.bfloat16
    i32 = mybir.dt.int32
    u32 = mybir.dt.uint32
    ALU = mybir.AluOpType
    ACT = mybir.ActivationFunctionType
    AX = mybir.AxisListType

    P = 128
    B, S, D = x.shape
    KC = D // P
    H = 16
    DH = D // H
    HD = S // H
    HALF = H // KC
    RG = 4
    EPS = 1e-5
    MASKED = -1e30
    ND = HD // 2 + 1
    WR = ND - 2
    YW = HD + WR
    KW = HD + ND - 1
    NPR = ND * HD
    F = gate_w.shape[1]
    FM = F // P
    NE = down_embed.shape[0]
    EC = NE // P
    NK = keys.shape[2]
    TK = 8
    NT = B
    G = 2
    TG = NT // G
    LOWEST = -3.0e38

    es = ExitStack()
    with es:
        def sb(name, shape, dt=fp32):
            return es.enter_context(nc.sbuf_tensor(name, shape, dt))

        def sem(name):
            return es.enter_context(nc.semaphore(name))

        def over(ap, at, shape, dt=fp32):
            step = [1]
            for m in reversed(shape[2:]):
                step.insert(0, step[0] * m)
            v = bass.AP(ap.tensor, ap.offset + at, [list(ap.ap[0])] + [[a, m] for a, m in zip(step, shape[1:])])
            assert at + step[0] * shape[1] <= int(np.prod(ap.shape[1:]))
            return v if dt == fp32 else v.bitcast(dt)

        x_sb = sb("x_sb", [P, B, D])
        xb_sb = sb("xb_sb", [P, B, D])
        c_sb = sb("c_sb", [P, B, D])
        w_sb = {n: sb(f"w_{n}", [P, KC, D]) for n in ("q", "k", "v", "o")}
        g_col = sb("g_col", [P, KC])
        b_col = sb("b_col", [P, KC])
        bq_col = sb("bq_col", [P, KC])
        bk_col = sb("bk_col", [P, KC])
        bv_row = sb("bv_row", [P, D])
        bo_row = sb("bo_row", [P, D])
        skip_row = sb("skip_row", [P, H])
        toep = sb("toep", [P, H, D])
        wqr_sb = sb("wqr_sb", [P, KC, P])
        key_sb = sb("key_sb", [P, 2, NK])
        gate_sb = sb("gate_sb", [P, KC, F])
        up_sb = sb("up_sb", [P, KC, F])
        down_sb = sb("down_sb", [P, FM, D])
        de_sb = sb("de_sb", [P, EC, D])
        deT = sb("deT", [P, KC, NE])
        ue_sb = sb("ue_sb", [P, EC, D])
        ident = sb("ident", [P, P])
        anti = sb("anti", [P, P])
        ident_bf = sb("ident_bf", [P, P], bf16)
        ones_bf = sb("ones_bf", [P, P], bf16)
        mask_qk = sb("mask_qk", [P, P], bf16)
        mask_kq = sb("mask_kq", [P, P], bf16)
        zeros_bf = sb("zeros_bf", [P, P], bf16)
        head_sel = sb("head_sel", [P, 2])
        power = sb("power", [P, B])
        iota_i = sb("iota_i", [P, NK], i32)
        iota_f = sb("iota_f", [P, NK])

        stat1 = sb("stat1", [P, B, 6])
        mv1 = sb("mv1", [P, B, 2])
        var1 = sb("var1", [P, B])
        rstd1 = sb("rstd1", [P, B])
        xh = sb("xh", [P, 2, D])
        xnT = sb("xnT", [P, 2, KC, P])
        qT = sb("qT", [P, 2, KC, 2, P])
        kT = sb("kT", [P, 2, KC, P])
        qT_bf = sb("qT_bf", [P, KC, 2, P], bf16)
        kT_bf = sb("kT_bf", [P, KC, P], bf16)
        vext = sb("vext", [P, 2, H, DH + 1])
        negmax = sb("negmax", [P, RG, KC, 2], bf16)
        shift = sb("shift", [P, RG, KC * 2, P], bf16)
        shift32 = shift[:, :, :, :].rearrange("p r h q -> p (r h q)").bitcast(fp32)
        pT = sb("pT", [P, RG, KC, 2, P])
        rsum = sb("rsum", [P, H])
        av = sb("av", [P, D])
        avT = sb("avT", [P, KC, P])
        res = sb("res", [P, D])
        stat2 = sb("stat2", [P, 6])
        mv2 = sb("mv2", [P, 2])
        var2 = sb("var2", [P, 1])
        rstd2 = sb("rstd2", [P, 1])
        x1 = sb("x1", [P, B, D])

        kk = sb("kk", [P, KC, H, B, KW])
        kv = sb("kv", [P, 2, KC, 2, B, ND, HD])
        Y = sb("Y", [P, KC, H, B, ND, YW])
        QW = WR + HD + ND - 1
        qq = over(toep[:, :, :], 0, [P, 2, KC, H, QW])
        z = [over(pT[:, :, :, :, :], 0, [P, KC, TK, H, HD]),
             over(kv[:, :, :, :, :, :, :], 0, [P, KC, TK, H, HD])]
        res2 = over(shift32, 0, [P, 2, D])
        stat3 = sb("stat3", [P, 6])
        mv3 = sb("mv3", [P, 2])
        var3 = sb("var3", [P, 1])
        rstd3 = sb("rstd3", [P, 1])
        x2 = xb_sb
        x2T = over(c_sb[:, :, :], 0, [P, KC, B, P])
        qm_home = x_sb[:, :, :]
        qm = over(qm_home, 0, [P, 2 * B * P])

        rt = over(kk[:, :, :, :, :], 0, [P, NT, 2, NK])
        v8 = sb("v8", [P, NT, 2, TK])
        i8 = sb("i8", [P, NT, 2, TK], u32)
        f8 = sb("f8", [P, NT, 2, TK])
        fx64 = sb("fx64", [P, NT, TK])
        pair = over(kk[:, :, :, :, :], 1024, [P, NT, TK, TK])
        m8 = sb("m8", [P, NT, TK])
        pair_r = over(kk[:, :, :, :, :], 1536, [P, NT, TK, TK])
        sel = over(kk[:, :, :, :, :], 2048, [P, NT, TK, TK])
        ew = over(Y[:, :, :, :, :, :], 8192, [P, NT, TK, TK])
        tmp = over(kk[:, :, :, :, :], 2560, [P, NT, TK, TK])
        zs = sb("zs", [P, NT])
        rz = sb("rz", [P, NT])
        p511 = sb("p511", [P, NT])
        cnt = sb("cnt", [P, NT, TK])
        cx = sb("cx", [P, NT, TK])
        rk = over(qm_home, 0, [P, 2, TK, NK])
        rank = over(Y[:, :, :, :, :, :], 8704, [P, NT, NK])
        ex = sb("ex", [P, NT, TK])
        ey = over(Y[:, :, :, :, :, :], 9216, [P, NT, NK])
        hT = Y[:, :, :, :, :, :].rearrange("p a b c d e -> p (a b c d e)")[:, 0:FM * B * P].rearrange(
            "p (m t) -> p m t", m=FM)
        pd = toep[:, :, :].rearrange("p h l -> p (h l)").rearrange("p (t a b) -> p t a b", t=NT, a=TK)
        gs = over(Y[:, :, :, :, :, :], 9728, [P, 2, 512])
        es_t = over(Y[:, :, :, :, :, :], 10752, [P, 2, NE])
        cT = over(Y[:, :, :, :, :, :], 11776, [P, 2, EC, P])
        res4 = over(Y[:, :, :, :, :, :], 12800, [P, 2, D])
        stat4 = sb("stat4", [P, 6])
        mv4 = sb("mv4", [P, 2])
        var4 = sb("var4", [P, 1])
        rstd4 = sb("rstd4", [P, 1])
        y_out = over(Y[:, :, :, :, :, :], 13312, [P, 2, D])

        ps = es.enter_context(nc.psum_tensor("ps", [P, 8, 512], fp32))
        sc_ps = ps[:, 0:RG, :]
        xT_ps = ps[:, 4, 0:D].rearrange("p (c t) -> p c t", c=KC)
        K_ps = xT_ps
        Q_ps = ps[:, 5, 0:D].rearrange("p (c t) -> p c t", c=KC)
        V_ps = ps[:, 5, D:2 * D]
        PV_ps = ps[:, 6, 0:H * (DH + 1)].rearrange("p (h e) -> p h e", h=H)
        avT_ps = ps[:, 6, 0:D].rearrange("p (c t) -> p c t", c=KC)
        wo_ps = ps[:, 6, 0:D]
        CW = B * NPR
        conv_ps = ps[:, 7, 0:CW]

        names = """qkb_r crev_r l_x0 l_x1 l_g l_b l_bq l_bk l_bv l_bo l_skip l_toep l_ctx l_wq l_wk l_wv l_wo l_wqr l_key l_gate
        l_up l_down l_de l_ue consts id_r pool_o dve_o ones xb mv1_r var1_r rstd1_r ctxT kk_r toep_r kv_r conv_mm conv_ev y_r
        xh_r xT_r xnT_r kp_r qp0_r v_r q_r k_r vv_r sc_r max_r shift_r st_r p_r pv_r av_r avT_r avTs_r wo_r res_r var2_r
        rstd2_r x1_r x1T_r qq_r z_r red_r var3_r rstd3_r x2_r x2T_r x2Ts_r qp_r qm_r rt_r rts_r gu_r gs_r h_r
        ein_r ex_r pd_r ed_r es_r c_r cT_r cTs_r o_r var4_r rstd4_r yo_r stored f8_r cx_r rk_r rank_r pd1_r pd2_r pd3_r exz_r act_o deT_ps deT_r qm0""".split()
        s = {n: sem(n) for n in names}

        def view(ap, dims, off=0):
            return bass.AP(ap.tensor, ap.offset + off, [list(ap.ap[0])] + dims)

        def bc(ap, axis, n):
            a = ap.unsqueeze(axis)
            shape = list(a.shape)
            shape[axis] = n
            return a.to_broadcast(shape)

        blk = es.enter_context(nc.Block())

        @blk.sync
        def _(sp):
            xr = x.rearrange("b t d -> t b d")
            sp.dma_start(x_sb[:, 0:1, :], xr[:, 0:1, :]).then_inc(s["l_x0"], 16)
            for n, w in (("k", wk), ("q", wq), ("v", wv)):
                sp.dma_start(w_sb[n][:, :, :], w.rearrange("(c p) n -> p c n", p=P)).then_inc(s[f"l_w{n}"], 16)
            sp.dma_start(c_sb[:, :, :], ctx_in.rearrange("b t d -> t b d")).then_inc(s["l_ctx"], 16)
            sp.dma_start(x_sb[:, 1:B, :], xr[:, 1:B, :]).then_inc(s["l_x1"], 16)
            W = taps.shape[1]
            sp.dma_start(toep[:, :, :], bass.AP(taps.tensor, taps.offset, [[1, P], [W, H], [1, D]])
                         ).then_inc(s["l_toep"], 16)
            sp.dma_start(w_sb["o"][:, :, :], wo.rearrange("(c p) n -> p c n", p=P)).then_inc(s["l_wo"], 16)
            sp.dma_start(de_sb[:, :, :], down_embed.rearrange("(c p) n -> p c n", p=P)).then_inc(s["l_de"], 16)
            sp.dma_start(gate_sb[:, :, :], gate_w.rearrange("(c p) n -> p c n", p=P)).then_inc(s["l_gate"], 16)
            sp.dma_start(up_sb[:, :, :], up_w.rearrange("(c p) n -> p c n", p=P)).then_inc(s["l_up"], 16)
            sp.dma_start(down_sb[:, :, :], down_w.rearrange("(c p) n -> p c n", p=P)).then_inc(s["l_down"], 16)
            sp.dma_start(ue_sb[:, :, :], up_embed.rearrange("(c p) n -> p c n", p=P)).then_inc(s["l_ue"], 16)
            for t in range(NT):
                sp.wait_ge(s["yo_r"], t + 1)
                sp.dma_start(out[t, :, :], y_out[:, t % 2, :]).then_inc(s["stored"], 16)
                sp.wait_ge(s["stored"], 16 * (t + 1))

        @blk.gpsimd
        def _(pool):
            n = [0]

            def link(ins):
                n[0] += 1
                ins.then_inc(s["pool_o"], 1)
                pool.wait_ge(s["pool_o"], n[0])

            link(nc.gpsimd.memset(ident[:, :], 0.0))
            nc.gpsimd.affine_select(out=ident[:, :], in_=ident[:, :], compare_op=ALU.not_equal, fill=1.0, base=0,
                                    pattern=[[-1, P]], channel_multiplier=1).then_inc(s["id_r"], 1)
            link(nc.gpsimd.memset(anti[:, :], 0.0))
            nc.gpsimd.affine_select(out=anti[:, :], in_=anti[:, :], compare_op=ALU.not_equal, fill=1.0, base=1 - P,
                                    pattern=[[1, P]], channel_multiplier=1).then_inc(s["id_r"], 1)
            link(nc.gpsimd.memset(power[:, :], -0.5))
            nc.gpsimd.memset(ones_bf[:, :], 1.0).then_inc(s["consts"], 1)
            pool.wait_ge(s["var1_r"], 1)
            nc.gpsimd.tensor_tensor(rstd1[:, 0:1], var1[:, 0:1], power[:, 0:1], ALU.pow).then_inc(s["rstd1_r"], 1)
            link(nc.gpsimd.memset(zeros_bf[:, :], 0.0))
            nc.gpsimd.affine_select(out=mask_qk[:, :], in_=zeros_bf[:, :], compare_op=ALU.is_ge, fill=MASKED,
                                    base=0, pattern=[[-1, P]], channel_multiplier=1).then_inc(s["consts"], 1)
            nc.gpsimd.affine_select(out=mask_kq[:, :], in_=zeros_bf[:, :], compare_op=ALU.is_ge, fill=MASKED,
                                    base=0, pattern=[[1, P]], channel_multiplier=-1).then_inc(s["consts"], 1)
            pool.wait_ge(s["id_r"], 1)
            nc.gpsimd.tensor_copy(ident_bf[:, :], ident[:, :]).then_inc(s["consts"], 1)
            pool.wait_ge(s["var1_r"], 2)
            nc.gpsimd.tensor_tensor(rstd1[:, 1:B], var1[:, 1:B], power[:, 1:B], ALU.pow).then_inc(s["rstd1_r"], 1)
            nc.gpsimd.memset(vext[:, :, :, DH:DH + 1], 1.0).then_inc(s["ones"], 1)
            pool.wait_ge(s["kk_r"], B)
            kkw = kk[:, :, :, :, :].rearrange("p c h b i -> p (c h b) i")
            nc.gpsimd.tensor_copy(kkw[:, :, HD:KW], kkw[:, :, 0:KW - HD]).then_inc(s["kk_r"], 1)
            pool.wait_ge(s["l_bo"], 16)
            nc.gpsimd.tensor_tensor(xb_sb[:, :, :], x_sb[:, :, :], bc(bo_row[:, :], 1, B), ALU.add
                                    ).then_inc(s["xb"], 1)
            nc.gpsimd.iota(iota_i[:, :], pattern=[[1, NK]], base=0, channel_multiplier=0).then_inc(s["pool_o"], 1)
            n[0] += 1
            pool.wait_ge(s["pool_o"], n[0])
            nc.gpsimd.tensor_copy(iota_f[:, :], iota_i[:, :]).then_inc(s["consts"], 1)

            def attn_rstd(b):
                pool.wait_ge(s["var2_r"], b + 1)
                nc.gpsimd.tensor_tensor(rstd2[:, :], var2[:, :], power[:, 0:1], ALU.pow).then_inc(s["rstd2_r"], 1)

            for b in range(B):
                for r in range(RG):
                    pool.wait_ge(s["max_r"], RG * b + r + 1)
                    if b >= 1:
                        pool.wait_ge(s["st_r"], 2 * (b - 1) + r // 2 + 1)
                    nc.gpsimd.tensor_tensor(shift[:, r, :, :], bc(ident_bf[:, :], 1, KC * 2),
                                            bc(negmax[:, r, :, :].rearrange("p t e -> p (t e)"), 2, P), ALU.mult
                                            ).then_inc(s["shift_r"], 1)
                if b >= 1:
                    attn_rstd(b - 1)
                pool.wait_ge(s["conv_ev"], 2 * KC * (b + 1))
                for c in range(KC):
                    yv = Y[:, c, 2 * b:2 * b + 2, :, 1:1 + WR, :].rearrange("p h b d i -> p (h b) d i")
                    nc.gpsimd.tensor_copy(yv[:, :, :, 0:WR], yv[:, :, :, HD:YW]).then_inc(s["y_r"], 1)
            pool.wait_ge(s["xh_r"], B)
            nc.gpsimd.memset(qm, 0.0).then_inc(s["qm0"], 1)
            attn_rstd(B - 1)
            for b in range(B):
                pool.wait_ge(s["var3_r"], b + 1)
                nc.gpsimd.tensor_tensor(rstd3[:, :], var3[:, :], power[:, 0:1], ALU.pow).then_inc(s["rstd3_r"], 1)
            def ranks(t):
                if t == 0:
                    pool.wait_ge(s["f8_r"], 1)
                if t >= 2:
                    pool.wait_ge(s["rank_r"], t - 1)
                for k in range(TK):
                    nc.gpsimd.tensor_scalar(rk[:, t % 2, k, :], iota_f[:, :], f8[:, t, 1, k:k + 1], float(TK - k),
                                            ALU.is_equal, ALU.mult).then_inc(s["rk_r"], 1)

            def rank_and_count(t):
                pool.wait_ge(s["rank_r"], t + 1)
                if t == 0:
                    pool.wait_ge(s["cx_r"], 1)
                nc.gpsimd.tensor_tensor(pd[:, t, :, :], bc(rank[:, t, :], 1, TK), bc(cx[:, t, :], 2, NK), ALU.add
                                        ).then_inc(s["pd1_r"], 1)

            def weigh(t):
                pool.wait_ge(s["pd2_r"], t + 1)
                if t == 0:
                    pool.wait_ge(s["exz_r"], 1)
                nc.gpsimd.tensor_tensor(pd[:, t, :, :], pd[:, t, :, :], bc(ex[:, t, :], 2, NK), ALU.mult
                                        ).then_inc(s["pd3_r"], 1)

            def last_rstd(t):
                pool.wait_ge(s["var4_r"], t + 1)
                nc.gpsimd.tensor_tensor(rstd4[:, :], var4[:, :], power[:, 0:1], ALU.pow).then_inc(s["rstd4_r"], 1)

            ranks(0)
            ranks(1)
            rank_and_count(0)
            ranks(2)
            weigh(0)
            for t in range(NT):
                if t + 1 < NT:
                    rank_and_count(t + 1)
                if t + 3 < NT:
                    ranks(t + 3)
                if t + 1 < NT:
                    weigh(t + 1)
                if t >= 1:
                    last_rstd(t - 1)
            last_rstd(NT - 1)

        @blk.scalar
        def _(act):
            for n, t, src in (("g", g_col, ln_g), ("b", b_col, ln_b), ("bq", bq_col, bq), ("bk", bk_col, bk)):
                act.dma_start(t[:, :], src.rearrange("(c p) -> p c", p=P),
                              allow_slow_non_contiguous=True).then_inc(s[f"l_{n}"], 16)
            act.dma_start(bv_row[:, :], bv.partition_broadcast(P)).then_inc(s["l_bv"], 16)
            act.dma_start(skip_row[:, :], skip.partition_broadcast(P)).then_inc(s["l_skip"], 16)
            act.dma_start(bo_row[:, :], bo.partition_broadcast(P)).then_inc(s["l_bo"], 16)
            act.dma_start(wqr_sb[:, :, :], w_query.rearrange("(c p) n -> p c n", p=P)).then_inc(s["l_wqr"], 16)
            for e in range(2):
                act.dma_start(key_sb[64 * e:64 * e + 64, :, :], keys.rearrange("t d k -> d t k")
                              ).then_inc(s["l_key"], 16)

            def norm_cols(b):
                act.wait_ge(s["xT_r"], b + 1)
                if b == 0:
                    act.wait_ge(s["l_g"], 16)
                    act.wait_ge(s["l_b"], 16)
                if b >= 2:
                    act.wait_ge(s["v_r"], b - 1)
                for c in range(KC):
                    nc.scalar.activation(xnT[:, b % 2, c, :], xT_ps[:, c, :], ACT.Identity, bias=b_col[:, c:c + 1],
                                         scale=g_col[:, c:c + 1]).then_inc(s["xnT_r"], 1)

            def k_cols(b):
                act.wait_ge(s["kp_r"], b + 1)
                if b == 0:
                    act.wait_ge(s["l_bk"], 16)
                if b >= 2:
                    act.wait_ge(s["st_r"], 2 * (b - 1))
                for c in range(KC):
                    nc.scalar.activation(kT[:, b % 2, c, :], K_ps[:, c, :], ACT.Identity, bias=bk_col[:, c:c + 1]
                                         ).then_inc(s["k_r"], 1)

            def rounded_cols(b):
                act.wait_ge(s["q_r"], 2 * KC * (b + 1))
                act.wait_ge(s["k_r"], KC * (b + 1))
                if b >= 1:
                    act.wait_ge(s["sc_r"], b)
                nc.scalar.copy(kT_bf[:, :, :], kT[:, b % 2, :, :]).then_inc(s["qkb_r"], 1)
                nc.scalar.copy(qT_bf[:, :, :, :].rearrange("p c e t -> p (c e t)"),
                               qT[:, b % 2, :, :, :].rearrange("p c e t -> p (c e t)")).then_inc(s["qkb_r"], 1)

            def probs(b, r):
                act.wait_ge(s["st_r"], 2 * b + r // 2 + 1)
                if b >= 1:
                    act.wait_ge(s["pv_r"], RG * (b - 1) + r + 1)
                nc.scalar.activation(pT[:, r, :, :, :].rearrange("p t e q -> p (t e q)"), sc_ps[:, r, :], ACT.Exp
                                     ).then_inc(s["p_r"], 1)

            def conv_out(h, c):
                act.wait_ge(s["conv_mm"], KC * h + c + 1)
                nc.scalar.copy(Y[:, c, h, :, :, WR:YW].rearrange("p b d i -> p (b d) i"),
                               conv_ps.rearrange("p (b i) -> p b i", i=HD)).then_inc(s["conv_ev"], 1)

            norm_cols(0)
            k_cols(0)
            rounded_cols(0)
            act.wait_ge(s["l_ctx"], 16)
            nc.scalar.copy(x1[:, :, :], view(c_sb[:, :, :], [[D, B], [-1, D]], D - 1)).then_inc(s["crev_r"], 1)
            for b in range(B):
                act.wait_ge(s["ctxT"], b + 1)
                nc.scalar.copy(kk[:, :, :, b, 0:HD], ps[:, b % 4, 0:D].rearrange("p (c h i) -> p c h i", c=KC, h=H)
                               ).then_inc(s["kk_r"], 1)

            for b in range(B):
                conv_out(2 * b, 0)
                if b >= 1:
                    act.wait_ge(s["avT_r"], b)
                    nc.scalar.copy(avT[:, :, :], avT_ps).then_inc(s["avTs_r"], 1)
                if b + 1 < B:
                    norm_cols(b + 1)
                    k_cols(b + 1)
                probs(b, 0)
                probs(b, 1)
                conv_out(2 * b, 1)
                probs(b, 2)
                probs(b, 3)
                conv_out(2 * b + 1, 0)
                if b + 1 < B:
                    rounded_cols(b + 1)
                conv_out(2 * b + 1, 1)
            act.wait_ge(s["avT_r"], B)
            nc.scalar.copy(avT[:, :, :], avT_ps).then_inc(s["avTs_r"], 1)

            act.wait_ge(s["deT_ps"], 1)
            for c in range(KC):
                nc.scalar.copy(deT[:, c, :], ps[:, c, :]).then_inc(s["deT_r"], 1)

            def cross_query_rows(b):
                act.wait_ge(s["x1T_r"], b + 1)
                if b >= 2:
                    act.wait_ge(s["z_r"], 2 * KC * (b - 1))
                src = ps[:, 2 + b % 2, 0:D].rearrange("p (c h i) -> p (c h) i", c=KC, h=H)
                dst = qq[:, b % 2, :, :, :].rearrange("p c h i -> p (c h) i")
                nc.scalar.copy(dst[:, :, WR:WR + HD], src).then_inc(s["qq_r"], 1)
                nc.scalar.copy(dst[:, :, WR + HD:QW], src[:, :, 0:ND - 1]).then_inc(s["qq_r"], 1)
                nc.scalar.copy(dst[:, :, 0:WR], src[:, :, HD - WR:HD]).then_inc(s["qq_r"], 1)

            def x2_cols(b):
                act.wait_ge(s["x2T_r"], b + 1)
                nc.scalar.copy(x2T[:, :, b, :], ps[:, 6, 0:D].rearrange("p (c t) -> p c t", c=KC)
                               ).then_inc(s["x2Ts_r"], 1)

            def route_cols(b):
                act.wait_ge(s["qp_r"], b + 1)
                if b == 0:
                    act.wait_ge(s["qm0"], 1)
                cols = qm[:, 2 * P * b:2 * P * (b + 1)].rearrange("p (t e) -> p t e", e=2)
                for e in range(2):
                    nc.scalar.copy(cols[64 * e:64 * e + 64, :, e], ps[64 * e:64 * e + 64, 7, 0:P]
                                   ).then_inc(s["qm_r"], 1)

            cross_query_rows(0)
            cross_query_rows(1)
            for b in range(B):
                if b + 2 < B:
                    cross_query_rows(b + 2)
                if b >= 1:
                    x2_cols(b - 1)
                if b >= 2:
                    route_cols(b - 2)

            def gate_silu(u):
                act.wait_ge(s["gu_r"], u + 1)
                if u >= 2:
                    act.wait_ge(s["h_r"], u - 1)
                nc.scalar.activation(gs[:, u % 2, :], ps[:, 2 + 2 * (u % 3), :], ACT.Silu).then_inc(s["gs_r"], 1)

            gate_silu(0)
            x2_cols(B - 1)
            route_cols(B - 2)
            gate_silu(1)
            route_cols(B - 1)
            act.wait_ge(s["rt_r"], 1)
            for i in range(2):
                nc.scalar.copy(rt[:, 4 * i:4 * i + 4, :, :].rearrange("p t a k -> p (t a k)"), ps[:, i, :]
                               ).then_inc(s["rts_r"], 1)
            for u in range(2, G * FM):
                gate_silu(u)
                if u == 10:
                    act.wait_ge(s["ein_r"], 3)
                    nc.scalar.activation(ew[:, :, :, :].rearrange("p t a b -> p (t a b)"),
                                         ew[:, :, :, :].rearrange("p t a b -> p (t a b)"), ACT.Exp
                                         ).then_inc(s["ex_r"], 1)
                    nc.scalar.activation(ex[:, :, :], ex[:, :, :], ACT.Exp).then_inc(s["ex_r"], 1)
                    nc.scalar.activation(ey[:, :, :], ey[:, :, :], ACT.Exp).then_inc(s["ex_r"], 1)

            def gate_expert(t):
                act.wait_ge(s["ed_r"], t + 1)
                if t >= 2:
                    act.wait_ge(s["cT_r"], t - 1)
                nc.scalar.activation(es_t[:, t % 2, :], ps[:, 6 + t % 2, :], ACT.Silu).then_inc(s["es_r"], 1)

            gate_expert(0)
            for t in range(NT):
                if t + 1 < NT:
                    gate_expert(t + 1)
                act.wait_ge(s["cT_r"], t + 1)
                if t >= 2:
                    act.wait_ge(s["o_r"], t - 1)
                nc.scalar.copy(cT[:, t % 2, :, :].rearrange("p c t -> p (c t)"), ps[:, 4 + t % 2, :]
                               ).then_inc(s["cTs_r"], 1)

        @blk.vector
        def _(dve):
            n = [0]

            def link(ins):
                n[0] += 1
                ins.then_inc(s["dve_o"], 1)
                dve.wait_ge(s["dve_o"], n[0])

            V = nc.vector

            def stats1(b):
                link(V.bn_stats(stat1[:, b, :], x_sb[:, b, :]))
                V.bn_aggr(mv1[:, b, :], stat1[:, b, :]).then_inc(s["mv1_r"], 1)

            def xhat(b):
                if b >= 2:
                    dve.wait_ge(s["xT_r"], b - 1)
                V.tensor_scalar(xh[:, b % 2, :], x_sb[:, b, :], mv1[:, b, 0:1], rstd1[:, b:b + 1], ALU.subtract,
                                ALU.mult).then_inc(s["xh_r"], 1)

            def kv_products(b):
                if b >= 2:
                    dve.wait_ge(s["conv_mm"], 2 * KC * (b - 1))
                for c in range(KC):
                    src = kk[:, c, 2 * b:2 * b + 2, :, 0:HD]
                    V.tensor_tensor(kv[:, b % 2, c, :, :, :, :].rearrange("p h b d i -> p (h b) d i"),
                                    view(src, [[KW, 2 * B], [0, ND], [1, HD]]),
                                    view(src, [[KW, 2 * B], [1, ND], [1, HD]]), ALU.mult).then_inc(s["kv_r"], 1)

            def q_cols(b):
                dve.wait_ge(s["qp0_r"], b + 1)
                if b >= 2:
                    dve.wait_ge(s["st_r"], 2 * (b - 1))
                for c in range(KC):
                    for e in range(2):
                        V.tensor_scalar(qT[:, b % 2, c, e, :], Q_ps[:, c, :], bq_col[:, c:c + 1],
                                        head_sel[:, e:e + 1], ALU.add, ALU.mult).then_inc(s["q_r"], 1)

            def v_rows(b):
                dve.wait_ge(s["v_r"], b + 1)
                if b >= 2:
                    dve.wait_ge(s["pv_r"], RG * (b - 1))
                V.tensor_tensor(vext[:, b % 2, :, 0:DH], V_ps.rearrange("p (h e) -> p h e", h=H),
                                bv_row[:, :].rearrange("p (h e) -> p h e", h=H), ALU.add).then_inc(s["vv_r"], 1)

            def row_max(b, r):
                if r == 0:
                    dve.wait_ge(s["sc_r"], b + 1)
                if b >= 1:
                    dve.wait_ge(s["shift_r"], RG * (b - 1) + r + 1)
                V.tensor_reduce(negmax[:, r, :, :].rearrange("p t e -> p (t e)"),
                                sc_ps[:, r, :].rearrange("p (h k) -> p h k", k=P), AX.X, ALU.max, negate=True
                                ).then_inc(s["max_r"], 1)

            def attn_norm(b):
                dve.wait_ge(s["pv_r"], RG * (b + 1))
                link(V.reciprocal(rsum[:, :], PV_ps[:, :, DH]))
                if b >= 1:
                    dve.wait_ge(s["avT_r"], b)
                V.tensor_tensor(av[:, :].rearrange("p (h e) -> p h e", h=H), PV_ps[:, :, 0:DH],
                                bc(rsum[:, :], 2, DH), ALU.mult).then_inc(s["av_r"], 1)

            def attn_res(b):
                dve.wait_ge(s["wo_r"], b + 1)
                if b == 0:
                    dve.wait_ge(s["xb"], 1)
                V.tensor_tensor(res[:, :], wo_ps, xb_sb[:, b, :], ALU.add).then_inc(s["res_r"], 1)
                dve.wait_ge(s["res_r"], b + 1)
                link(V.bn_stats(stat2[:, :], res[:, :]))
                link(V.bn_aggr(mv2[:, :], stat2[:, :]))
                V.tensor_scalar(var2[:, :], mv2[:, 1:2], EPS, None, ALU.add).then_inc(s["var2_r"], 1)

            def attn_out(b):
                dve.wait_ge(s["rstd2_r"], b + 1)
                V.tensor_scalar(x1[:, b, :], res[:, :], mv2[:, 0:1], rstd2[:, :], ALU.subtract, ALU.mult
                                ).then_inc(s["x1_r"], 1)

            dve.wait_ge(s["l_x0"], 16)
            stats1(0)
            dve.wait_ge(s["mv1_r"], 1)
            V.tensor_scalar(var1[:, 0:1], mv1[:, 0, 1:2], EPS, None, ALU.add).then_inc(s["var1_r"], 1)
            dve.wait_ge(s["id_r"], 1)
            for e in range(2):
                link(V.tensor_reduce(head_sel[:, e:e + 1],
                                     ident[:, :].rearrange("p (g e i) -> p g e i", g=RG, e=2)[:, :, e, :],
                                     AX.XY, ALU.add))
            link(V.tensor_scalar(head_sel[:, :], head_sel[:, :], float(DH) ** -0.5, None, ALU.mult))
            dve.wait_ge(s["rstd1_r"], 1)
            xhat(0)
            dve.wait_ge(s["l_bq"], 16)
            q_cols(0)
            dve.wait_ge(s["l_bv"], 16)
            v_rows(0)
            dve.wait_ge(s["l_x1"], 16)
            for b in range(1, B):
                stats1(b)
            dve.wait_ge(s["mv1_r"], B)
            V.tensor_scalar(var1[:, 1:B], mv1[:, 1:B, 1], EPS, None, ALU.add).then_inc(s["var1_r"], 1)
            dve.wait_ge(s["rstd1_r"], 2)
            xhat(1)
            dve.wait_ge(s["l_toep"], 16)
            dve.wait_ge(s["l_skip"], 16)
            dve.wait_ge(s["id_r"], 2)
            dtmp = Y[:, 0, :, :, :, :].rearrange("p h b d i -> p (h b d i)")[:, 0:H * P].rearrange(
                "p (h l) -> p h l", h=H)
            link(V.tensor_tensor(dtmp, bc(anti[:, :], 1, H), bc(skip_row[:, :], 2, P), ALU.mult))
            V.tensor_tensor(toep[:, :, 0:P], toep[:, :, 0:P], dtmp, ALU.add).then_inc(s["toep_r"], 1)
            dve.wait_ge(s["toep_r"], 1)
            dve.wait_ge(s["kk_r"], B + 1)
            kv_products(0)

            for b in range(B):
                if b >= 1:
                    attn_norm(b - 1)
                for r in range(RG):
                    row_max(b, r)
                if b + 1 < B:
                    kv_products(b + 1)
                if b >= 1:
                    attn_res(b - 1)
                if b + 1 < B:
                    q_cols(b + 1)
                if b >= 1:
                    attn_out(b - 1)
                if b + 1 < B:
                    v_rows(b + 1)
                if b + 2 < B:
                    xhat(b + 2)
            attn_norm(B - 1)
            attn_res(B - 1)
            attn_out(B - 1)

            def cross_products(b, c):
                if c == 0:
                    dve.wait_ge(s["qq_r"], 3 * (b + 1))
                    if b == 0:
                        dve.wait_ge(s["y_r"], KC * B)
                    if b >= 2:
                        dve.wait_ge(s["red_r"], b - 1)
                row = B * ND * YW
                yb = Y[:, c, :, b, :, :]
                q0 = qq[:, b % 2, c, :, :]
                V.tensor_tensor(z[b % 2][:, c, 0:ND, :, :], view(yb, [[YW, ND], [row, H], [1, HD]], WR),
                                view(q0, [[1, ND], [QW, H], [1, HD]], WR), ALU.mult).then_inc(s["z_r"], 1)
                V.tensor_tensor(z[b % 2][:, c, ND:TK, :, :], view(yb, [[YW - 1, WR], [row, H], [1, HD]], YW + WR - 1),
                                view(q0, [[-1, WR], [QW, H], [1, HD]], WR - 1), ALU.mult).then_inc(s["z_r"], 1)

            def cross_res(b):
                dve.wait_ge(s["red_r"], b + 1)
                r = res2[:, b % 2, :]
                link(V.tensor_tensor(r, ps[:, 4 + b % 2, 0:D], x1[:, b, :], ALU.add))
                link(V.bn_stats(stat3[:, :], r))
                link(V.bn_aggr(mv3[:, :], stat3[:, :]))
                V.tensor_scalar(var3[:, :], mv3[:, 1:2], EPS, None, ALU.add).then_inc(s["var3_r"], 1)

            def cross_out(b):
                dve.wait_ge(s["rstd3_r"], b + 1)
                V.tensor_scalar(x2[:, b, :], res2[:, b % 2, :], mv3[:, 0:1], rstd3[:, :], ALU.subtract, ALU.mult
                                ).then_inc(s["x2_r"], 1)

            for b in range(2):
                for c in range(KC):
                    cross_products(b, c)
            for b in range(B):
                cross_res(b)
                if b + 2 < B:
                    cross_products(b + 2, 0)
                cross_out(b)
                if b + 2 < B:
                    cross_products(b + 2, 1)

            def hidden(u):
                dve.wait_ge(s["gs_r"], u + 1)
                g, m = divmod(u, FM)
                V.tensor_tensor(hT[:, m, 512 * g:512 * (g + 1)], ps[:, 3 + 2 * (u % 3), :], gs[:, u % 2, :], ALU.mult
                                ).then_inc(s["h_r"], 1)

            hidden(0)
            hidden(1)
            dve.wait_ge(s["rts_r"], 2)
            dve.wait_ge(s["consts"], 5)
            for u in range(NT):
                if u >= 2:
                    hidden(u)
                link(V.max(v8[:, u, 0, :], rt[:, u, 0, :]))
                link(V.max(v8[:, u, 1, :], rt[:, u, 1, :]))
                link(V.max_index(i8[:, u, 0, :], v8[:, u, 0, :], rt[:, u, 0, :]))
                link(V.max_index(i8[:, u, 1, :], v8[:, u, 1, :], rt[:, u, 1, :]))
            link(V.tensor_tensor(pair[:, :, :, :], bc(v8[:, :, 0, :], 3, TK), bc(v8[:, :, 1, :], 2, TK), ALU.add))
            V.tensor_copy(f8[:, :, :, :], i8[:, :, :, :]).then_inc(s["f8_r"], 1)
            dve.wait_ge(s["f8_r"], 1)
            hidden(8)
            for t in range(NT):
                pr = pair[:, t, :, :].rearrange("p a b -> p (a b)")
                link(V.max(m8[:, t, :], pr))
                link(V.match_replace(pair_r[:, t, :, :].rearrange("p a b -> p (a b)"), m8[:, t, :], pr, LOWEST))
            hidden(9)
            V.tensor_tensor(ew[:, :, :, :].rearrange("p t a b -> p t (a b)"),
                            pair[:, :, :, :].rearrange("p t a b -> p t (a b)"), bc(m8[:, :, 0], 2, TK * TK),
                            ALU.subtract).then_inc(s["ein_r"], 1)
            V.tensor_tensor(ex[:, :, :], rt[:, :, 0, 0:TK], bc(v8[:, :, 0, 0], 2, TK), ALU.subtract
                            ).then_inc(s["ein_r"], 1)
            V.tensor_tensor(ey[:, :, :], rt[:, :, 1, :], bc(v8[:, :, 1, 0], 2, NK), ALU.subtract
                            ).then_inc(s["ein_r"], 1)
            link(V.tensor_tensor(sel[:, :, :, :], pair_r[:, :, :, :], pair[:, :, :, :], ALU.not_equal))
            link(V.tensor_reduce(cnt[:, :, :], sel[:, :, :, :], AX.X, ALU.add))
            hidden(10)
            link(V.tensor_tensor(tmp[:, :, :, :], bc(f8[:, :, 0, :], 2, TK),
                                 view(iota_f[:, 0:TK], [[0, NT], [1, TK], [0, TK]]), ALU.is_equal))
            link(V.tensor_tensor(tmp[:, :, :, :], tmp[:, :, :, :], bc(cnt[:, :, :], 2, TK), ALU.mult))
            V.tensor_reduce(cx[:, :, :], tmp[:, :, :, :], AX.X, ALU.add).then_inc(s["cx_r"], 1)
            dve.wait_ge(s["cx_r"], 1)
            hidden(11)
            dve.wait_ge(s["ex_r"], 3)
            link(V.tensor_tensor(ew[:, :, :, :], ew[:, :, :, :], sel[:, :, :, :], ALU.mult))
            hidden(12)
            link(V.tensor_reduce(zs[:, :], ew[:, :, :, :], AX.XY, ALU.add))
            link(V.reciprocal(rz[:, :], zs[:, :]))
            link(V.tensor_scalar(fx64[:, :, :], f8[:, :, 0, :], float(NK), None, ALU.mult))
            link(V.tensor_tensor(tmp[:, :, :, :], bc(fx64[:, :, :], 3, TK), bc(f8[:, :, 1, :], 2, TK), ALU.add))
            fl = "p t a b -> p (t a b)"
            link(V.scalar_tensor_tensor(tmp[:, :, :, :].rearrange(fl), tmp[:, :, :, :].rearrange(fl), float(NE - 1),
                                        ew[:, :, :, :].rearrange(fl), ALU.is_ge, ALU.mult))
            link(V.tensor_reduce(p511[:, :], tmp[:, :, :, :], AX.XY, ALU.add))
            link(V.tensor_tensor(p511[:, :], p511[:, :], rz[:, :], ALU.mult))
            V.tensor_tensor(ex[:, :, :], ex[:, :, :], bc(rz[:, :], 2, TK), ALU.mult).then_inc(s["exz_r"], 1)
            hidden(13)

            def rank_sum(t):
                dve.wait_ge(s["rk_r"], TK * (t + 1))
                V.tensor_reduce(rank[:, t, :], view(rk[:, t % 2, :, :], [[1, NK], [NK, TK]]), AX.X, ALU.add
                                ).then_inc(s["rank_r"], 1)

            def select(t):
                dve.wait_ge(s["pd1_r"], t + 1)
                V.scalar_tensor_tensor(pd[:, t, :, :], pd[:, t, :, :], TK + 0.5, bc(ey[:, t, :], 1, TK),
                                       ALU.is_gt, ALU.mult).then_inc(s["pd2_r"], 1)

            def combine(t):
                dve.wait_ge(s["pd3_r"], t + 1)
                link(V.tensor_copy(pd[:, t, TK - 1, NK - 1:NK], p511[:, t:t + 1]))
                dve.wait_ge(s["es_r"], t + 1)
                V.tensor_tensor(es_t[:, t % 2, :], es_t[:, t % 2, :], pd[:, t, :, :].rearrange("p a b -> p (a b)"),
                                ALU.mult).then_inc(s["c_r"], 1)

            rank_sum(0)
            rank_sum(1)
            hidden(14)
            select(0)
            rank_sum(2)
            hidden(15)

            def last_norm(t):
                dve.wait_ge(s["o_r"], t + 1)
                r = res4[:, t % 2, :]
                link(V.tensor_tensor(r, ps[:, t % 2, 0:D], x2[:, t, :], ALU.add))
                link(V.bn_stats(stat4[:, :], r))
                link(V.bn_aggr(mv4[:, :], stat4[:, :]))
                V.tensor_scalar(var4[:, :], mv4[:, 1:2], EPS, None, ALU.add).then_inc(s["var4_r"], 1)
                dve.wait_ge(s["rstd4_r"], t + 1)
                if t >= 2:
                    dve.wait_ge(s["stored"], 16 * (t - 1))
                V.tensor_scalar(y_out[:, t % 2, :], r, mv4[:, 0:1], rstd4[:, :], ALU.subtract, ALU.mult
                                ).then_inc(s["yo_r"], 1)

            for t in range(NT):
                if t + 1 < NT:
                    select(t + 1)
                if t + 3 < NT:
                    rank_sum(t + 3)
                combine(t)
                if t >= 1:
                    last_norm(t - 1)
            last_norm(NT - 1)

        @blk.tensor
        def _(pe):
            M = nc.tensor.matmul
            T = nc.tensor.transpose

            def x_transpose(b):
                pe.wait_ge(s["xh_r"], b + 1)
                if b >= 1:
                    pe.wait_ge(s["k_r"], KC * b)
                for c in range(KC):
                    last = T(xT_ps[:, c, :], xh[:, b % 2, c * P:(c + 1) * P], ident[:, :])
                last.then_inc(s["xT_r"], 1)

            def project(b):
                pe.wait_ge(s["xnT_r"], KC * (b + 1))
                if b == 0:
                    pe.wait_ge(s["l_wq"], 16)
                    pe.wait_ge(s["l_wk"], 16)
                    pe.wait_ge(s["l_wv"], 16)
                if b >= 1:
                    pe.wait_ge(s["vv_r"], b)
                for w, dst, done in (("k", K_ps, "kp_r"), ("q", Q_ps, "qp0_r")):
                    for c in range(KC):
                        for k in range(KC):
                            last = M(dst[:, c, :], w_sb[w][:, k, c * P:(c + 1) * P], xnT[:, b % 2, k, :],
                                     start=(k == 0), stop=(k == KC - 1))
                    last.then_inc(s[done], 1)

            def project_values(b):
                pe.wait_ge(s["q_r"], 2 * KC * (b + 1))
                for k in range(KC):
                    last = M(V_ps, xnT[:, b % 2, k, :], w_sb["v"][:, k, :], start=(k == 0), stop=(k == KC - 1))
                last.then_inc(s["v_r"], 1)

            def scores(b):
                pe.wait_ge(s["qkb_r"], 2 * (b + 1))
                if b >= 1:
                    pe.wait_ge(s["p_r"], RG * b)
                for r in range(RG):
                    M(sc_ps[:, r, :], ident_bf[:, :], bc(mask_qk[:, :], 1, 4), start=True,
                      stop=False)
                for t in range(KC):
                    for e in range(2):
                        for r in range(RG):
                            i = 2 * t + e
                            last = M(sc_ps[:, r, i * P:(i + 1) * P], qT_bf[32 * r:32 * r + 32, t, e, :],
                                     kT_bf[32 * r:32 * r + 32, t, :], start=False, stop=(i == 3))
                last.then_inc(s["sc_r"], 1)

            def scores_t(b, half):
                pe.wait_ge(s["shift_r"], RG * b + 2 * half + 2)
                rr = range(2 * half, 2 * half + 2)
                for r in rr:
                    M(sc_ps[:, r, :], ident_bf[:, :], bc(mask_kq[:, :], 1, 4), start=True,
                      stop=False)
                    M(sc_ps[:, r, :], ones_bf[:, :], shift[:, r, :, :].rearrange("p e q -> p (e q)"), start=False,
                      stop=False)
                for t in range(KC):
                    for r in rr:
                        last = M(sc_ps[:, r, 2 * t * P:2 * (t + 1) * P], kT[32 * r:32 * r + 32, b % 2, t, :],
                                 qT[32 * r:32 * r + 32, b % 2, t, :, :].rearrange("p e q -> p (e q)"), start=False,
                                 stop=(t == KC - 1))
                last.then_inc(s["st_r"], 1)

            def values(b, r):
                pe.wait_ge(s["p_r"], RG * b + r + 1)
                pe.wait_ge(s["vv_r"], b + 1)
                if b == 0:
                    pe.wait_ge(s["ones"], 1)
                if b >= 1:
                    pe.wait_ge(s["res_r"], b)
                for t in range(KC):
                    for e in range(2):
                        h = t * HALF + 2 * r + e
                        last = M(PV_ps[:, h, :], pT[:, r, t, e, :], vext[:, b % 2, h, :], start=True, stop=True)
                last.then_inc(s["pv_r"], 1)

            def out_project(b):
                pe.wait_ge(s["av_r"], b + 1)
                if b == 0:
                    pe.wait_ge(s["l_wo"], 16)
                for c in range(KC):
                    last = T(avT_ps[:, c, :], av[:, c * P:(c + 1) * P], ident[:, :])
                last.then_inc(s["avT_r"], 1)

            def out_project2(b):
                pe.wait_ge(s["avTs_r"], b + 1)
                for c in range(KC):
                    last = M(wo_ps, avT[:, c, :], w_sb["o"][:, c, :], start=(c == 0), stop=(c == KC - 1))
                last.then_inc(s["wo_r"], 1)

            def conv(h, c):
                pe.wait_ge(s["kv_r"], KC * (h // 2 + 1))
                if h == 0:
                    pe.wait_ge(s["toep_r"], 1)
                i = KC * h + c
                if i >= 1:
                    pe.wait_ge(s["conv_ev"], i)
                for k in range(c + 1):
                    d = c - k
                    last = M(conv_ps, toep[:, h, d * P:(d + 1) * P],
                             kv[:, h // 2 % 2, k, h % 2, :, :, :].rearrange("p b d i -> p (b d i)"), start=(k == 0),
                             stop=(k == c))
                last.then_inc(s["conv_mm"], 1)

            pe.wait_ge(s["id_r"], 1)
            x_transpose(0)
            project(0)
            project_values(0)
            pe.wait_ge(s["crev_r"], 1)
            for b in range(B):
                if b >= 4:
                    pe.wait_ge(s["kk_r"], b - 3)
                for c in range(KC):
                    last = T(ps[:, b % 4, c * P:(c + 1) * P], x1[:, b, (KC - 1 - c) * P:(KC - c) * P], ident[:, :])
                last.then_inc(s["ctxT"], 1)
            pe.wait_ge(s["kk_r"], B)
            pe.wait_ge(s["consts"], 4)
            for b in range(B):
                scores(b)
                conv(2 * b, 0)
                if b >= 1:
                    out_project(b - 1)
                if b + 1 < B:
                    x_transpose(b + 1)
                if b >= 1:
                    out_project2(b - 1)
                if b + 1 < B:
                    project(b + 1)
                scores_t(b, 0)
                conv(2 * b, 1)
                scores_t(b, 1)
                values(b, 0)
                conv(2 * b + 1, 0)
                values(b, 1)
                if b + 1 < B:
                    project_values(b + 1)
                values(b, 2)
                conv(2 * b + 1, 1)
                values(b, 3)
            out_project(B - 1)
            out_project2(B - 1)

            pe.wait_ge(s["l_de"], 16)
            pe.wait_ge(s["p_r"], RG * B)
            for c in range(KC):
                for e in range(EC):
                    last = T(ps[:, c, e * P:(e + 1) * P], de_sb[:, e, c * P:(c + 1) * P], ident[:, :])
            last.then_inc(s["deT_ps"], 1)

            def cross_queries(b):
                pe.wait_ge(s["x1_r"], b + 1)
                if b >= 2:
                    pe.wait_ge(s["qq_r"], 3 * (b - 1))
                for c in range(KC):
                    last = T(ps[:, 2 + b % 2, c * P:(c + 1) * P], x1[:, b, c * P:(c + 1) * P], ident[:, :])
                last.then_inc(s["x1T_r"], 1)

            def cross_sum(b):
                pe.wait_ge(s["z_r"], 2 * KC * (b + 1))
                if b >= 2:
                    pe.wait_ge(s["x2_r"], b - 1)
                for c in range(KC):
                    for t in range(TK):
                        last = M(ps[:, 4 + b % 2, c * P:(c + 1) * P], z[b % 2][:, c, t, :, :].rearrange("p h j -> p (h j)"), ident[:, :],
                                 start=(t == 0), stop=(t == TK - 1))
                last.then_inc(s["red_r"], 1)

            def x2_transpose(b):
                pe.wait_ge(s["x2_r"], b + 1)
                if b >= 1:
                    pe.wait_ge(s["x2Ts_r"], b)
                for c in range(KC):
                    last = T(ps[:, 6, c * P:(c + 1) * P], x2[:, b, c * P:(c + 1) * P], ident[:, :])
                last.then_inc(s["x2T_r"], 1)

            def route_query(b):
                pe.wait_ge(s["x2Ts_r"], b + 1)
                if b >= 1:
                    pe.wait_ge(s["qm_r"], 2 * b)
                else:
                    pe.wait_ge(s["l_wqr"], 16)
                for c in range(KC):
                    last = M(ps[:, 7, 0:P], wqr_sb[:, c, :], x2T[:, c, b, :], start=(c == 0), stop=(c == KC - 1))
                last.then_inc(s["qp_r"], 1)

            cross_queries(0)
            cross_queries(1)
            for b in range(B):
                if b + 2 < B:
                    cross_queries(b + 2)
                cross_sum(b)
                if b >= 1:
                    x2_transpose(b - 1)
                if b >= 2:
                    route_query(b - 2)
            def gate_up(u):
                g, m = divmod(u, FM)
                if u == 0:
                    pe.wait_ge(s["l_gate"], 16)
                    pe.wait_ge(s["l_up"], 16)
                if u == 1:
                    pe.wait_ge(s["x2_r"], B)
                if u == 2:
                    pe.wait_ge(s["qm_r"], 2 * B)
                if u >= 3:
                    pe.wait_ge(s["h_r"], u - 2)
                for a, w in enumerate((gate_sb, up_sb)):
                    for k in range(KC):
                        last = M(ps[:, 2 + 2 * (u % 3) + a, :], w[:, k, m * P:(m + 1) * P],
                                 x2T[:, k, TG * g:TG * (g + 1), :].rearrange("p b t -> p (b t)"), start=(k == 0),
                                 stop=(k == KC - 1))
                last.then_inc(s["gu_r"], 1)

            gate_up(0)
            x2_transpose(B - 1)
            route_query(B - 2)
            gate_up(1)
            route_query(B - 1)

            pe.wait_ge(s["deT_r"], KC)
            pe.wait_ge(s["qm_r"], 2 * B)
            pe.wait_ge(s["l_key"], 32)
            for t in range(NT):
                for a in range(2):
                    c0 = (t % 4) * 2 * NK + a * NK
                    col = (a * NT + t) * P
                    last = M(ps[:, t // 4, c0:c0 + NK], qm[:, col:col + P], key_sb[:, a, :], start=True, stop=True)
            last.then_inc(s["rt_r"], 1)

            for u in range(2, G * FM):
                gate_up(u)

            def expert_in(t):
                if t >= 2:
                    pe.wait_ge(s["es_r"], t - 1)
                for k in range(KC):
                    last = M(ps[:, 6 + t % 2, :], x2T[:, k, t, :], deT[:, k, :], start=(k == 0), stop=(k == KC - 1))
                last.then_inc(s["ed_r"], 1)

            pe.wait_ge(s["h_r"], G * FM)
            pe.wait_ge(s["rts_r"], 2)
            pe.wait_ge(s["l_down"], 16)
            pe.wait_ge(s["l_ue"], 16)
            expert_in(0)
            for t in range(NT):
                if t + 1 < NT:
                    expert_in(t + 1)
                pe.wait_ge(s["c_r"], t + 1)
                if t >= 2:
                    pe.wait_ge(s["cTs_r"], t - 1)
                for e in range(EC):
                    last = T(ps[:, 4 + t % 2, e * P:(e + 1) * P], es_t[:, t % 2, e * P:(e + 1) * P], ident[:, :])
                last.then_inc(s["cT_r"], 1)
                if t >= 2:
                    pe.wait_ge(s["yo_r"], t - 1)
                for m in range(FM):
                    M(ps[:, t % 2, 0:D], hT[:, m, t * P:(t + 1) * P], down_sb[:, m, :], start=(m == 0), stop=False)
                pe.wait_ge(s["cTs_r"], t + 1)
                for e in range(EC):
                    last = M(ps[:, t % 2, 0:D], cT[:, t % 2, e, :], ue_sb[:, e, :], start=False, stop=(e == EC - 1))
                last.then_inc(s["o_r"], 1)


def kernel(**inputs):
    import numpy as np
    import concourse.bacc as bacc
    from concourse.bass_utils import run_bass_kernel_spmd

    names = ['x', 'ctx_2048', 'L0_attn_ln_g', 'L0_attn_ln_b', 'L0_attn_Wq', 'L0_attn_bq', 'L0_attn_Wk', 'L0_attn_bk',
             'L0_attn_Wv', 'L0_attn_bv', 'L0_attn_Wo', 'L0_attn_bo', 'L0_xattn_ssm_kernel', 'L0_xattn_D',
             'L0_ffn_W_q', 'L0_ffn_keys', 'L0_ffn_down_embed', 'L0_ffn_up_embed', 'L0_ffn_gate_w', 'L0_ffn_up_w',
             'L0_ffn_down_w']
    nc = bacc.Bacc("TRN2", target_bir_lowering=False, num_devices=1)
    arrays, args = {}, []
    for name in names:
        a = np.ascontiguousarray(inputs[name])
        if name == 'L0_xattn_ssm_kernel':
            padded = np.zeros((a.shape[0], 127 + a.shape[1]), a.dtype)
            padded[:, 127:] = a
            a = padded
        arrays[f"in_{name}"] = a
        args.append(nc.dram_tensor(f"in_{name}", a.shape, mybir.dt.from_np(a.dtype), kind="ExternalInput").ap())
    shape = tuple(inputs['x'].shape)
    args.append(nc.dram_tensor("out_0", shape, mybir.dt.float32, kind="ExternalOutput").ap())
    decoder_layer(nc, *args)
    r = run_bass_kernel_spmd(nc, [arrays], core_ids=[0])
    return r.results[0]["out_0"]
```

```python
import concourse.bass as bass
from concourse import mybir
from contextlib import ExitStack

import numpy as np


def decoder_layer(nc, x, ctx_in, wq, wk, wv, wo, taps, w_query, keys, down_embed, up_embed, gate_w, up_w, down_w,
                  cols, rows, out):
    fp32 = mybir.dt.float32
    f32r = mybir.dt.float32r
    bf16 = mybir.dt.bfloat16
    i32 = mybir.dt.int32
    u32 = mybir.dt.uint32
    ALU = mybir.AluOpType
    ACT = mybir.ActivationFunctionType
    AX = mybir.AxisListType

    P = 128
    B, S, D = x.shape
    KC = D // P
    H = 16
    DH = D // H
    HD = S // H
    HALF = H // KC
    RG = 4
    EPS = 1e-5
    MASKED = -1e30
    ND = HD // 2 + 1
    WR = ND - 2
    YW = HD + WR
    KW = HD + ND - 1
    NPR = ND * HD
    F = gate_w.shape[1]
    FM = F // P
    NE = down_embed.shape[1]
    EC = NE // P
    NK = keys.shape[2]
    TK = 8
    NT = B
    G = 2
    TG = NT // G
    LOWEST = -3.0e38
    WARM = 12
    RANKS_AT = 10
    TG4 = H // 4

    es = ExitStack()
    with es:
        where = {}

        def sb(name, shape, dt=fp32):
            t = es.enter_context(nc.sbuf_tensor(name, shape, dt))
            where[name] = nc.sbuf_base - int(np.prod(shape[1:])) * (2 if dt == bf16 else 4)
            return t

        def sem(name):
            return es.enter_context(nc.semaphore(name))

        def over(ap, at, shape, dt=fp32):
            step = [1]
            for m in reversed(shape[2:]):
                step.insert(0, step[0] * m)
            v = bass.AP(ap.tensor, ap.offset + at, [list(ap.ap[0])] + [[a, m] for a, m in zip(step, shape[1:])])
            assert at + step[0] * shape[1] <= int(np.prod(ap.shape[1:]))
            return v if dt == fp32 else v.bitcast(dt)

        def at(name, home, off, shape, dt=fp32):
            return nc.alloc_sbuf_tensor_at(name, shape, dt, offset=where[home] + 4 * off)

        FIRST_SPLIT = 2

        x_sb = sb("x_sb", [P, B, D])
        xb_sb = sb("xb_sb", [P, B, D])
        x2T_hi = sb("x2T_hi", [P, KC, B, P], f32r)
        w_sb = {n: sb(f"w_{n}", [P, KC, D]) for n in ("q", "k", "v", "o")}
        col_sb = sb("col_sb", [P, 4, KC])
        g_col, b_col, bq_col, bk_col = (col_sb[:, i, :] for i in range(4))
        row_sb = sb("row_sb", [P, 2 * D + H])
        bv_row, bo_row, skip_row = row_sb[:, 0:D], row_sb[:, D:2 * D], row_sb[:, 2 * D:2 * D + H]
        toep = sb("toep", [P, H, D])
        wqr_sb = sb("wqr_sb", [P, KC, P])
        key_sb = sb("key_sb", [P, 2, NK])
        gate_sb = sb("gate_sb", [P, KC, F])
        up_sb = sb("up_sb", [P, KC, F])
        down_sb = sb("down_sb", [P, FM, D])
        ue_sb = sb("ue_sb", [P, EC, D])
        wv_hi = at("wv_hi", "gate_sb", 0, [P, KC, D], f32r)
        wv_lo = at("wv_lo", "gate_sb", 512, [P, KC, D], f32r)
        xnT_hi = at("xnT_hi", "gate_sb", 1024, [P, 2, KC, P], f32r)
        xnT_lo = at("xnT_lo", "gate_sb", 1536, [P, 2, KC, P], f32r)
        qT_hi = at("qT_hi", "down_sb", 0, [P, 2, KC, 2, P], f32r)
        qT_lo = at("qT_lo", "down_sb", 1024, [P, 2, KC, 2, P], f32r)
        kT_hi = at("kT_hi", "ue_sb", 0, [P, 2, KC, P], f32r)
        kT_lo = at("kT_lo", "ue_sb", 512, [P, 2, KC, P], f32r)
        deT = sb("deT", [P, KC, NE])
        ident = sb("ident", [P, P])
        anti = sb("anti", [P, P])
        ident_bf = sb("ident_bf", [P, P], bf16)
        ones_bf = sb("ones_bf", [P, P], bf16)
        mask_qk = sb("mask_qk", [P, P], bf16)
        zeros_bf = sb("zeros_bf", [P, P], bf16)
        head_sel = sb("head_sel", [P, 2])
        power = sb("power", [P, B])
        iota_i = sb("iota_i", [P, NK], i32)
        iota_f = sb("iota_f", [P, NK])

        xh = sb("xh", [P, 2, D])
        xnT = sb("xnT", [P, 2, KC, P])
        qT = sb("qT", [P, 2, KC, 2, P])
        kT = sb("kT", [P, 2, KC, P])
        qT_bf = sb("qT_bf", [P, KC, 2, P], bf16)
        kT_bf = sb("kT_bf", [P, KC, P], bf16)
        vext = sb("vext", [P, 2, H, DH + 1])
        shift = sb("shift", [P, RG, KC * 2, P], bf16)
        av = sb("av", [P, D])
        avT = sb("avT", [P, KC, P])
        res = sb("res", [P, D])
        negmax = sb("negmax", [P, RG, KC, 2], bf16)
        stat1 = sb("stat1", [P, B, 6])
        mv1 = sb("mv1", [P, B, 2])
        var1 = sb("var1", [P, B])
        rstd1 = sb("rstd1", [P, B])
        rsum = sb("rsum", [P, H])
        stat2 = sb("stat2", [P, 6])
        mv2 = sb("mv2", [P, 2])
        var2 = sb("var2", [P, 1])
        rstd2 = sb("rstd2", [P, 1])

        Y = sb("Y", [P, KC, H, B, ND, YW])
        pT = sb("pT", [P, RG, KC, 2, P])
        kv = sb("kv", [P, 2, KC, 2, B, ND, HD])
        x1 = sb("x1", [P, B, D])
        kk = sb("kk", [P, KC, H, B, KW])
        QW = WR + HD + ND - 1
        qq = at("qq", "kT", 0, [P, 2, KC, H, QW])
        z = [over(pT[:, :, :, :, :], 0, [P, KC, TK, H, HD]),
             over(kv[:, :, :, :, :, :, :], 0, [P, KC, TK, H, HD])]
        res2 = at("res2", "kT", 960, [P, 2, D])
        stat3 = sb("stat3", [P, 6])
        mv3 = sb("mv3", [P, 2])
        var3 = sb("var3", [P, 1])
        rstd3 = sb("rstd3", [P, 1])
        x2 = xb_sb
        x2T = at("x2T", "av", 96, [P, 2, KC, P])
        x2T_lo = at("x2T_lo", "w_q", 0, [P, KC, B, P], f32r)
        qm = at("qm", "x_sb", 0, [P, 2 * B * P])

        FT = FM * B * P
        pd = at("pd", "Y", 2 * FT, [P, NT, TK, NK])
        rt = at("rt", "kk", 2048, [P, NT, 2, NK])
        v8 = sb("v8", [P, NT, 2, TK])
        i8 = sb("i8", [P, NT, 2, TK], u32)
        f8 = sb("f8", [P, NT, 2, TK])
        fx64 = sb("fx64", [P, NT, TK])
        pair = over(pd[:, :, :, :], 4 * 512, [P, NT, TK, TK])
        m8 = sb("m8", [P, NT, TK])
        pair_r = over(pd[:, :, :, :], 5 * 512, [P, NT, TK, TK])
        sel = over(pd[:, :, :, :], 6 * 512, [P, NT, TK, TK])
        ew = at("ew", "deT", 0, [P, NT, TK, TK])
        tmp = over(pd[:, :, :, :], 7 * 512, [P, NT, TK, TK])
        zs = sb("zs", [P, NT])
        rz = sb("rz", [P, NT])
        p511 = sb("p511", [P, NT])
        cnt = sb("cnt", [P, NT, TK])
        cx = sb("cx", [P, NT, TK])
        rk = at("rk", "x_sb", 0, [P, NT, TK, NK], bf16)
        rank = at("rank", "deT", 512, [P, NT, NK])
        ex = sb("ex", [P, NT, TK])
        ey = at("ey", "av", 96, [P, NT, NK])
        hT_hi = at("hT_hi", "Y", 0, [P, FM, B * P], f32r)
        hT_lo = at("hT_lo", "Y", FT, [P, FM, B * P], f32r)
        gs = at("gs", "kT", 0, [P, 3, 512])
        deT_hi = sb("deT_hi", [P, KC, NE], f32r)
        deT_lo = at("deT_lo", "kT", 1536, [P, KC, NE], f32r)
        W1 = KC * F
        gate_hi = at("gate_hi", "toep", 0, [P, KC, F], f32r)
        gate_lo = at("gate_lo", "toep", W1, [P, KC, F], f32r)
        up_hi = at("up_hi", "gate_sb", 0, [P, KC, F], f32r)
        up_lo = at("up_lo", "xh", 0, [P, KC, F], f32r)
        down_hi = at("down_hi", "up_sb", 0, [P, FM, D], f32r)
        down_lo = at("down_lo", "kk", 0, [P, FM, D], f32r)
        ue_hi = at("ue_hi", "down_sb", 0, [P, EC, D], f32r)
        ue_lo = at("ue_lo", "down_sb", EC * D, [P, EC, D], f32r)
        es_t = at("es_t", "toep", 0, [P, 2, NE])
        cT_hi = at("cT_hi", "toep", 1024, [P, 2, EC, P], f32r)
        cT_lo = at("cT_lo", "toep", 2048, [P, 2, EC, P], f32r)
        y_out = at("y_out", "toep", 3072, [P, 2, D])
        res4 = at("res4", "toep", 3584, [P, 2, D])
        stat4 = sb("stat4", [P, 6])
        mv4 = sb("mv4", [P, 2])
        var4 = sb("var4", [P, 1])
        rstd4 = sb("rstd4", [P, 1])

        ps = es.enter_context(nc.psum_tensor("ps", [P, 8, 512], fp32))
        sc_ps = ps[:, 0:RG, :]
        xT_ps = ps[:, 4, 0:D].rearrange("p (c t) -> p c t", c=KC)
        K_ps = xT_ps
        Q_ps = ps[:, 5, 0:D].rearrange("p (c t) -> p c t", c=KC)
        V_ps = ps[:, 5, D:2 * D]
        PV_ps = ps[:, 6, 0:H * (DH + 1)].rearrange("p (h e) -> p h e", h=H)
        avT_ps = ps[:, 6, 0:D].rearrange("p (c t) -> p c t", c=KC)
        wo_ps = ps[:, 6, 0:D]
        CW = B * NPR
        conv_ps = ps[:, 7, 0:CW]

        names = []
        names += ("loaded_x0 loaded_x1 loaded_cols loaded_rows loaded_toep0 loaded_toep1 loaded_toep2 loaded_toep3 "
                  "loaded_ctx0 loaded_ctx1 loaded_wq loaded_wk loaded_wv loaded_wo loaded_wqr loaded_key "
                  "loaded_gate loaded_up loaded_down loaded_de loaded_ue").split()
        names += "stored".split()
        names += "gpsimd_done vector_done".split()
        names += "identity_ready consts_ready ones_column_ready".split()
        names += ("moments1_ready var1_ready rstd1_ready xhat_ready xT_in_psum xnT_ready xnT_hi_ready xnT_lo_ready "
                  "x_bias_ready").split()
        names += ("wv_hi_ready wv_lo_ready K_in_psum Q_in_psum V_in_psum kT_ready qT_ready values_ready "
                  "rounded_ready kT_hi_ready kT_lo_ready qT_hi_ready qT_lo_ready").split()
        names += ("scores_in_psum max_ready shift_ready shift1_ready scoresT_in_psum exp_ready probs_ready "
                  "PV_in_psum av_ready avT_in_psum avT_ready wo_in_psum").split()
        names += "residual2_ready var2_ready rstd2_ready x1_ready".split()
        names += "toep_ready kv_ready conv_in_psum Y_ready Y_wrapped".split()
        names += ("x1T_in_psum queries_ready terms_ready terms_paired sum_in_psum var3_ready rstd3_ready x2_ready "
                  "x2T_in_psum x2T_ready x2T_lo_ready").split()
        names += "deT_hi_ready deT_lo_ready weights_hi_ready weights_lo_ready ue_lo_ready".split()
        names += ("route_queries_zeroed route_query_in_psum route_queries_ready route_scores_in_psum "
                  "route_scores_ready best_keys_ready exp_arguments_ready expert_exp_ready ex_scaled counts_ready "
                  "rank_rows_ready rank_in_psum rank_ready rank_plus_count_ready selected_ready weighted_ready").split()
        names += ("gate_up_in_psum silu_ready hidden_ready hidden_hi_ready hidden_lo_ready "
                  "hidden_lo_ready_gpsimd").split()
        names += ("expert_in_psum expert_silu_ready expert_weighted cT_in_psum cT_hi_ready cT_lo_ready out_in_psum "
                  "var4_ready rstd4_ready y_ready").split()
        s = {n: sem(n) for n in names}

        def piece(w, i):
            return w[:, :, :].rearrange("p c n -> p (c n)")[:, 512 * i:512 * (i + 1)]

        wide = [(piece(gate_sb, i), piece(gate_hi, i), piece(gate_lo, i)) for i in range(4)] + [
            (piece(up_sb, i), piece(up_hi, i), piece(up_lo, i)) for i in range(4)] + [
            (piece(down_sb, i), piece(down_hi, i), piece(down_lo, i)) for i in range(4)] + [
            (piece(ue_sb, i), piece(ue_hi, i), piece(ue_lo, i)) for i in range(2)]
        NW = len(wide)
        NP = NW - 2

        def wide_at(b):
            return (b + 2,) if b < B - 1 else tuple(range(b + 2, NP))

        pool_units = (5, 7, 9, 11, 12)

        def wait_low(eng, u):
            on_pool = sum(v <= u for v in pool_units)
            eng.wait_ge(s["hidden_lo_ready"], u + 1 - on_pool)
            if on_pool:
                eng.wait_ge(s["hidden_lo_ready_gpsimd"], on_pool)

        def view(ap, dims, off=0):
            return bass.AP(ap.tensor, ap.offset + off, [list(ap.ap[0])] + dims)

        def bc(ap, axis, n):
            a = ap.unsqueeze(axis)
            shape = list(a.shape)
            shape[axis] = n
            return a.to_broadcast(shape)

        blk = es.enter_context(nc.Block())

        @blk.sync
        def _(sp):
            xr = x.rearrange("b t d -> t b d")
            def chunks(w):
                return w.rearrange("(c p) n -> p c n", p=P)

            sp.dma_start(x_sb[:, 0:2, :], xr[:, 0:2, :]).then_inc(s["loaded_x0"], 16)
            for n, w in (("k", wk), ("q", wq), ("v", wv)):
                sp.dma_start(w_sb[n][:, :, :], chunks(w)).then_inc(s[f"loaded_w{n}"], 16)
            sp.dma_start(kk[:, :, 0:4, :, :], ctx_in[:, :, 0:4, :, :]).then_inc(s["loaded_ctx0"], 16)
            W = taps.shape[1]
            for g in range(TG4):
                h0 = 4 * g
                sp.dma_start(toep[:, h0:h0 + 4, :], bass.AP(taps.tensor, taps.offset + h0 * W, [[1, P], [W, 4], [1, D]])
                             ).then_inc(s[f"loaded_toep{g}"], 16)
                if g == 0:
                    sp.dma_start(kk[:, :, 4:H, :, :], ctx_in[:, :, 4:H, :, :]).then_inc(s["loaded_ctx1"], 16)
                    sp.dma_start(x_sb[:, 2:B, :], xr[:, 2:B, :]).then_inc(s["loaded_x1"], 16)
                    sp.dma_start(w_sb["o"][:, :, :], chunks(wo)).then_inc(s["loaded_wo"], 16)
            sp.dma_start(wqr_sb[:, :, :], chunks(w_query)).then_inc(s["loaded_wqr"], 16)
            for e in range(2):
                sp.dma_start(key_sb[64 * e:64 * e + 64, :, :], keys.rearrange("t d k -> d t k")
                             ).then_inc(s["loaded_key"], 16)
            sp.dma_start(deT[:, :, :], chunks(down_embed)).then_inc(s["loaded_de"], 16)
            sp.wait_ge(s["V_in_psum"], B)
            sp.dma_start(gate_sb[:, :, :], chunks(gate_w)).then_inc(s["loaded_gate"], 16)
            sp.dma_start(up_sb[:, :, :], chunks(up_w)).then_inc(s["loaded_up"], 16)
            sp.wait_ge(s["scoresT_in_psum"], 2 * B)
            sp.dma_start(down_sb[:, :, :], chunks(down_w)).then_inc(s["loaded_down"], 16)
            sp.dma_start(ue_sb[:, :, :], chunks(up_embed)).then_inc(s["loaded_ue"], 16)
            for t in range(NT):
                sp.wait_ge(s["y_ready"], t + 1)
                sp.dma_start(out[t, :, :], y_out[:, t % 2, :]).then_inc(s["stored"], 16)
                sp.wait_ge(s["stored"], 16 * (t + 1))

        @blk.gpsimd
        def _(pool):
            n = [0]

            def link(ins):
                n[0] += 1
                ins.then_inc(s["gpsimd_done"], 1)
                pool.wait_ge(s["gpsimd_done"], n[0])

            nc.gpsimd.memset(ones_bf[:, :], 1.0).then_inc(s["consts_ready"], 1)
            link(nc.gpsimd.memset(ident[:, :], 0.0))
            nc.gpsimd.affine_select(out=ident[:, :], in_=ident[:, :], compare_op=ALU.not_equal, fill=1.0, base=0,
                                    pattern=[[-1, P]], channel_multiplier=1).then_inc(s["identity_ready"], 1)
            link(nc.gpsimd.memset(anti[:, :], 0.0))
            nc.gpsimd.affine_select(out=anti[:, :], in_=anti[:, :], compare_op=ALU.not_equal, fill=1.0, base=1 - P,
                                    pattern=[[1, P]], channel_multiplier=1).then_inc(s["identity_ready"], 1)
            link(nc.gpsimd.memset(power[:, :], -0.5))
            pool.wait_ge(s["var1_ready"], 1)
            nc.gpsimd.tensor_tensor(rstd1[:, 0:2], var1[:, 0:2], power[:, 0:2], ALU.pow).then_inc(s["rstd1_ready"], 1)
            link(nc.gpsimd.memset(zeros_bf[:, :], 0.0))
            nc.gpsimd.affine_select(out=mask_qk[:, :], in_=zeros_bf[:, :], compare_op=ALU.is_ge, fill=MASKED,
                                    base=0, pattern=[[-1, P]], channel_multiplier=1).then_inc(s["consts_ready"], 1)
            pool.wait_ge(s["identity_ready"], 1)
            nc.gpsimd.tensor_copy(ident_bf[:, :], ident[:, :]).then_inc(s["consts_ready"], 1)
            nc.gpsimd.memset(vext[:, :, :, DH:DH + 1], 1.0).then_inc(s["ones_column_ready"], 1)

            def low(out, full, hi, hi_ready, lo_ready):
                pool.wait_ge(*hi_ready)
                nc.gpsimd.tensor_tensor(out, full, hi, ALU.subtract).then_inc(s[lo_ready], 1)

            def keys_queries_low(b):
                if b >= 2:
                    pool.wait_ge(s["scoresT_in_psum"], 2 * (b - 1))
                i = b % 2
                low(kT_lo[:, i, :, :], kT[:, i, :, :], kT_hi[:, i, :, :], (s["kT_hi_ready"], b + 1), "kT_lo_ready")
                fl = "p c e t -> p (c e t)"
                low(qT_lo[:, i, :, :, :].rearrange(fl), qT[:, i, :, :, :].rearrange(fl),
                    qT_hi[:, i, :, :, :].rearrange(fl), (s["qT_hi_ready"], b + 1), "qT_lo_ready")

            def norm_low(b):
                if b >= FIRST_SPLIT + 2:
                    pool.wait_ge(s["V_in_psum"], b - 1)
                i = b % 2
                low(xnT_lo[:, i, :, :], xnT[:, i, :, :], xnT_hi[:, i, :, :], (s["xnT_hi_ready"], b - FIRST_SPLIT + 1),
                    "xnT_lo_ready")

            def attn_rstd(b):
                pool.wait_ge(s["var2_ready"], b + 1)
                nc.gpsimd.tensor_tensor(rstd2[:, :], var2[:, :], power[:, 0:1], ALU.pow).then_inc(s["rstd2_ready"], 1)

            def wrap_products(b):
                pool.wait_ge(s["Y_ready"], 2 * KC * (b + 1))
                for c in range(KC):
                    yv = Y[:, c, 2 * b:2 * b + 2, :, 1:1 + WR, :].rearrange("p h b d i -> p (h b) d i")
                    nc.gpsimd.tensor_copy(yv[:, :, :, 0:WR], yv[:, :, :, HD:YW]).then_inc(s["Y_wrapped"], 1)

            keys_queries_low(0)
            for b in range(B):
                if FIRST_SPLIT <= b + 1 < B:
                    norm_low(b + 1)
                for r in (0, 2, 3):
                    pool.wait_ge(s["max_ready"], RG * b + r + 1)
                    if b >= 1:
                        pool.wait_ge(s["scoresT_in_psum"], 2 * (b - 1) + r // 2 + 1)
                    nc.gpsimd.tensor_tensor(shift[:, r, :, :], bc(ident_bf[:, :], 1, KC * 2),
                                            bc(negmax[:, r, :, :].rearrange("p t e -> p (t e)"), 2, P), ALU.mult
                                            ).then_inc(s["shift_ready"], 1)
                if b >= 1:
                    attn_rstd(b - 1)
                for r in range(RG):
                    pool.wait_ge(s["exp_ready"], RG * b + r + 1)
                    nc.gpsimd.affine_select(out=pT[:, r, :, :, :].rearrange("p t e q -> p (t e) q"),
                                            in_=pT[:, r, :, :, :].rearrange("p t e q -> p (t e) q"),
                                            compare_op=ALU.is_ge, fill=0.0, base=0, pattern=[[0, KC * 2], [1, P]],
                                            channel_multiplier=-1).then_inc(s["probs_ready"], 1)
                if b >= 1:
                    wrap_products(b - 1)
                if b == 0:
                    pool.wait_ge(s["var1_ready"], 2)
                    nc.gpsimd.tensor_tensor(rstd1[:, 2:B], var1[:, 2:B], power[:, 2:B], ALU.pow
                                            ).then_inc(s["rstd1_ready"], 1)
                    pool.wait_ge(s["loaded_rows"], 16)
                    link(nc.gpsimd.iota(iota_i[:, :], pattern=[[1, NK]], base=0, channel_multiplier=0))
                    nc.gpsimd.tensor_copy(iota_f[:, :], iota_i[:, :]).then_inc(s["consts_ready"], 1)
                nc.gpsimd.tensor_tensor(xb_sb[:, b, :], x_sb[:, b, :], bo_row[:, :], ALU.add
                                        ).then_inc(s["x_bias_ready"], 1)
                if b == 1:
                    low(wv_lo[:, :, :], w_sb["v"][:, :, :], wv_hi[:, :, :], (s["wv_hi_ready"], 1), "wv_lo_ready")
                if b + 1 < B:
                    keys_queries_low(b + 1)
            wrap_products(B - 1)
            pool.wait_ge(s["x_bias_ready"], B)
            pool.wait_ge(s["xhat_ready"], B)
            nc.gpsimd.memset(qm[:, :], 0.0).then_inc(s["route_queries_zeroed"], 1)

            def wide_low(i):
                pool.wait_ge(s["weights_hi_ready"], i + 1)
                w, hi, lo = wide[i]
                nc.gpsimd.tensor_tensor(lo, w, hi, ALU.subtract).then_inc(s["weights_lo_ready"], 1)

            def x2_low(b):
                pool.wait_ge(s["x2T_ready"], 2 * (b + 1))
                nc.gpsimd.tensor_tensor(x2T_lo[:, :, b, :], x2T[:, b % 2, :, :], x2T_hi[:, :, b, :], ALU.subtract
                                        ).then_inc(s["x2T_lo_ready"], 1)

            def pair_terms(b, c):
                pool.wait_ge(s["terms_ready"], 2 * KC * b + 2 * (c + 1))
                last_two = [z[b % 2][:, c, t, :, :].rearrange("p h j -> p (h j)") for t in (TK - 2, TK - 1)]
                nc.gpsimd.tensor_tensor(last_two[0], last_two[0], last_two[1], ALU.add
                                        ).then_inc(s["terms_paired"], 1)

            for b in range(2):
                for c in range(KC):
                    pair_terms(b, c)
                if b == 0:
                    wide_low(0)
            attn_rstd(B - 1)
            wide_low(1)
            for b in range(B):
                pool.wait_ge(s["var3_ready"], b + 1)
                nc.gpsimd.tensor_tensor(rstd3[:, :], var3[:, :], power[:, 0:1], ALU.pow).then_inc(s["rstd3_ready"], 1)
                if b + 2 < B:
                    pair_terms(b + 2, 0)
                if 1 <= b < B - 1:
                    x2_low(b - 1)
                if b + 2 < B:
                    pair_terms(b + 2, 1)
                if b < B - 1:
                    wide_low(b + 2)
            for b in (B - 2, B - 1):
                wide_low(b + 3)
                x2_low(b)
            wide_low(NP - 1)
            fl = "p c e -> p (c e)"
            low(deT_lo[:, :, :].rearrange(fl), deT[:, :, :].rearrange(fl), deT_hi[:, :, :].rearrange(fl),
                (s["deT_hi_ready"], 1), "deT_lo_ready")

            def ranks(t):
                if t == 0:
                    pool.wait_ge(s["route_scores_in_psum"], 2)
                pool.wait_ge(s["best_keys_ready"], t + 1)
                for k in range(TK):
                    nc.gpsimd.tensor_scalar(rk[:, t, k, :], iota_f[:, :], f8[:, t, 1, k:k + 1], float(TK - k),
                                            ALU.is_equal, ALU.mult).then_inc(s["rank_rows_ready"], 1)

            def rank_and_count(t):
                pool.wait_ge(s["rank_ready"], t // 4 + 1)
                if t == 0:
                    pool.wait_ge(s["counts_ready"], 1)
                nc.gpsimd.tensor_tensor(pd[:, t, :, :], bc(rank[:, t, :], 1, TK), bc(cx[:, t, :], 2, NK), ALU.add
                                        ).then_inc(s["rank_plus_count_ready"], 1)

            def weigh(t):
                pool.wait_ge(s["selected_ready"], t + 1)
                if t == 0:
                    pool.wait_ge(s["ex_scaled"], 1)
                nc.gpsimd.tensor_tensor(pd[:, t, :, :], pd[:, t, :, :], bc(ex[:, t, :], 2, NK), ALU.mult
                                        ).then_inc(s["weighted_ready"], 1)

            def last_rstd(t):
                pool.wait_ge(s["var4_ready"], t + 1)
                nc.gpsimd.tensor_tensor(rstd4[:, :], var4[:, :], power[:, 0:1], ALU.pow).then_inc(s["rstd4_ready"], 1)

            def hidden_low(u):
                pool.wait_ge(s["hidden_hi_ready"], u + 1)
                g, m = divmod(u, FM)
                nc.gpsimd.tensor_tensor(hT_lo[:, m, 512 * g:512 * (g + 1)], gs[:, u % 3, :],
                                        hT_hi[:, m, 512 * g:512 * (g + 1)], ALU.subtract
                                        ).then_inc(s["hidden_lo_ready_gpsimd"], 1)

            for t in range(4):
                ranks(t)
            hidden_low(5)
            ranks(4)
            hidden_low(7)
            ranks(5)
            hidden_low(9)
            ranks(6)
            hidden_low(11)
            hidden_low(12)
            rank_and_count(0)
            rank_and_count(1)
            weigh(0)
            weigh(1)
            rank_and_count(2)
            for t in range(NT):
                if t + 2 < NT:
                    weigh(t + 2)
                if t == 0:
                    ranks(7)
                if t + 3 < NT:
                    rank_and_count(t + 3)
                if t >= 1:
                    last_rstd(t - 1)
            last_rstd(NT - 1)

        @blk.scalar
        def _(act):
            act.dma_start(col_sb[:, :, :], cols).then_inc(s["loaded_cols"], 16)
            act.dma_start(row_sb[:, :], rows.partition_broadcast(P)).then_inc(s["loaded_rows"], 16)

            def norm_cols(b):
                act.wait_ge(s["xT_in_psum"], b + 1)
                if b == 0:
                    act.wait_ge(s["loaded_cols"], 16)
                if b >= 2:
                    act.wait_ge(s["V_in_psum"], b - 1)
                for c in range(KC):
                    nc.scalar.activation(xnT[:, b % 2, c, :], xT_ps[:, c, :], ACT.Identity, bias=b_col[:, c:c + 1],
                                         scale=g_col[:, c:c + 1]).then_inc(s["xnT_ready"], 1)

            def norm_high(b):
                if b >= FIRST_SPLIT:
                    act.wait_ge(s["xnT_ready"], KC * (b + 1))
                    nc.scalar.copy(xnT_hi[:, b % 2, :, :], xnT[:, b % 2, :, :]).then_inc(s["xnT_hi_ready"], 1)

            def k_cols(b):
                act.wait_ge(s["K_in_psum"], b + 1)
                if b >= 2:
                    act.wait_ge(s["scoresT_in_psum"], 2 * (b - 1))
                for c in range(KC):
                    nc.scalar.activation(kT[:, b % 2, c, :], K_ps[:, c, :], ACT.Identity, bias=bk_col[:, c:c + 1]
                                         ).then_inc(s["kT_ready"], 1)

            def rounded_cols(b):
                act.wait_ge(s["qT_ready"], 2 * KC * (b + 1))
                act.wait_ge(s["kT_ready"], KC * (b + 1))
                if b >= 1:
                    act.wait_ge(s["scores_in_psum"], b)
                if b >= 2:
                    act.wait_ge(s["scoresT_in_psum"], 2 * (b - 1))
                nc.scalar.copy(kT_bf[:, :, :], kT[:, b % 2, :, :]).then_inc(s["rounded_ready"], 1)
                nc.scalar.copy(qT_bf[:, :, :, :].rearrange("p c e t -> p (c e t)"),
                               qT[:, b % 2, :, :, :].rearrange("p c e t -> p (c e t)")).then_inc(s["rounded_ready"], 1)
                nc.scalar.copy(kT_hi[:, b % 2, :, :], kT[:, b % 2, :, :]).then_inc(s["kT_hi_ready"], 1)
                nc.scalar.copy(qT_hi[:, b % 2, :, :, :].rearrange("p c e t -> p (c e t)"),
                               qT[:, b % 2, :, :, :].rearrange("p c e t -> p (c e t)")).then_inc(s["qT_hi_ready"], 1)

            def probs(b, r):
                act.wait_ge(s["scoresT_in_psum"], 2 * b + r // 2 + 1)
                if b >= 1:
                    act.wait_ge(s["PV_in_psum"], RG * (b - 1) + r + 1)
                nc.scalar.activation(pT[:, r, :, :, :].rearrange("p t e q -> p (t e q)"), sc_ps[:, r, :], ACT.Exp
                                     ).then_inc(s["exp_ready"], 1)

            def conv_out(h, c):
                act.wait_ge(s["conv_in_psum"], KC * h + c + 1)
                nc.scalar.copy(Y[:, c, h, :, :, WR:YW].rearrange("p b d i -> p (b d) i"),
                               conv_ps.rearrange("p (b i) -> p b i", i=HD)).then_inc(s["Y_ready"], 1)

            norm_cols(0)
            k_cols(0)
            rounded_cols(0)
            norm_cols(1)
            for b in range(B):
                if b >= 1:
                    act.wait_ge(s["avT_in_psum"], b)
                    nc.scalar.copy(avT[:, :, :], avT_ps).then_inc(s["avT_ready"], 1)
                    conv_out(2 * b, 0)
                if b + 1 < B:
                    k_cols(b + 1)
                for r in range(RG):
                    probs(b, r)
                if b == 0:
                    conv_out(0, 0)
                conv_out(2 * b, 1)
                conv_out(2 * b + 1, 0)
                conv_out(2 * b + 1, 1)
                if b + 1 < B:
                    rounded_cols(b + 1)
                if b + 2 < B:
                    norm_cols(b + 2)
                    norm_high(b + 2)
                if b == 0:
                    nc.scalar.copy(wv_hi[:, :, :], w_sb["v"][:, :, :]).then_inc(s["wv_hi_ready"], 1)
            def cross_query_rows(b):
                act.wait_ge(s["x1T_in_psum"], b + 1)
                if b >= 2:
                    act.wait_ge(s["terms_ready"], 2 * KC * (b - 1))
                src = ps[:, 2 + b % 2, 0:D].rearrange("p (c h i) -> p (c h) i", c=KC, h=H)
                dst = qq[:, b % 2, :, :, :].rearrange("p c h i -> p (c h) i")
                nc.scalar.copy(dst[:, :, WR:WR + HD], src).then_inc(s["queries_ready"], 1)
                nc.scalar.copy(dst[:, :, WR + HD:QW], src[:, :, 0:ND - 1]).then_inc(s["queries_ready"], 1)
                nc.scalar.copy(dst[:, :, 0:WR], src[:, :, HD - WR:HD]).then_inc(s["queries_ready"], 1)

            def x2_cols(b):
                act.wait_ge(s["x2T_in_psum"], b + 1)
                if b >= 2:
                    act.wait_ge(s["route_query_in_psum"], b - 1)
                    act.wait_ge(s["x2T_lo_ready"], b - 1)
                src = ps[:, 6, 0:D].rearrange("p (c t) -> p c t", c=KC)
                nc.scalar.copy(x2T[:, b % 2, :, :], src).then_inc(s["x2T_ready"], 1)
                nc.scalar.copy(x2T_hi[:, :, b, :], src).then_inc(s["x2T_ready"], 1)

            def wide_high(i):
                if i == 0:
                    act.wait_ge(s["loaded_gate"], 16)
                    act.wait_ge(s["loaded_up"], 16)
                if i % 4 == 0 and i:
                    act.wait_ge(s["weights_lo_ready"], i)
                if i == 8:
                    act.wait_ge(s["loaded_down"], 16)
                    act.wait_ge(s["loaded_ue"], 16)
                w, hi, lo = wide[i]
                nc.scalar.copy(hi, w).then_inc(s["weights_hi_ready"], 1)

            def route_cols(b):
                act.wait_ge(s["route_query_in_psum"], b + 1)
                if b == 0:
                    act.wait_ge(s["route_queries_zeroed"], 1)
                cols = qm[:, 2 * P * b:2 * P * (b + 1)].rearrange("p (t e) -> p t e", e=2)
                for e in range(2):
                    nc.scalar.copy(cols[64 * e:64 * e + 64, :, e], ps[64 * e:64 * e + 64, 7, 0:P]
                                   ).then_inc(s["route_queries_ready"], 1)

            def routing_scores(i):
                act.wait_ge(s["route_scores_in_psum"], i + 1)
                nc.scalar.copy(rt[:, 4 * i:4 * i + 4, :, :].rearrange("p t a k -> p (t a k)"), ps[:, i, :]
                               ).then_inc(s["route_scores_ready"], 1)

            cross_query_rows(0)
            act.wait_ge(s["avT_in_psum"], B)
            nc.scalar.copy(avT[:, :, :], avT_ps).then_inc(s["avT_ready"], 1)
            cross_query_rows(1)
            wide_high(0)
            wide_high(1)
            act.wait_ge(s["loaded_de"], 16)
            nc.scalar.copy(deT_hi[:, :, :], deT[:, :, :]).then_inc(s["deT_hi_ready"], 1)
            for b in range(B):
                if b + 2 < B:
                    cross_query_rows(b + 2)
                for i in wide_at(b):
                    wide_high(i)
                if b >= 1:
                    x2_cols(b - 1)
                if b >= 2:
                    route_cols(b - 2)

            def gate_silu(u):
                act.wait_ge(s["gate_up_in_psum"], u + 1)
                if u >= 3:
                    wait_low(act, u - 3)
                nc.scalar.activation(gs[:, u % 3, :], ps[:, 2 + 2 * (u % 3), :], ACT.Silu).then_inc(s["silu_ready"], 1)

            def hidden_high(u):
                act.wait_ge(s["hidden_ready"], u + 1)
                g, m = divmod(u, FM)
                nc.scalar.copy(hT_hi[:, m, 512 * g:512 * (g + 1)], gs[:, u % 3, :]).then_inc(s["hidden_hi_ready"], 1)

            gate_silu(0)
            x2_cols(B - 1)
            route_cols(B - 2)
            route_cols(B - 1)
            gate_silu(1)
            hidden_high(0)
            for i in range(NP, NW):
                wide_high(i)
            routing_scores(0)
            routing_scores(1)

            def ranks_out(i):
                act.wait_ge(s["rank_in_psum"], i + 1)
                nc.scalar.copy(rank[:, 4 * i:4 * i + 4, :].rearrange("p t k -> p (t k)"), ps[:, 2 * i, 0:4 * NK]
                               ).then_inc(s["rank_ready"], 1)

            for u in range(2, G * FM):
                gate_silu(u)
                if u == RANKS_AT + 1:
                    ranks_out(0)
                hidden_high(u - 1)
                if u == 10:
                    act.wait_ge(s["exp_arguments_ready"], 3)
                    nc.scalar.activation(ew[:, :, :, :].rearrange("p t a b -> p (t a b)"),
                                         ew[:, :, :, :].rearrange("p t a b -> p (t a b)"), ACT.Exp
                                         ).then_inc(s["expert_exp_ready"], 1)
                    nc.scalar.activation(ex[:, :, :], ex[:, :, :], ACT.Exp).then_inc(s["expert_exp_ready"], 1)
                    nc.scalar.activation(ey[:, :, :], ey[:, :, :], ACT.Exp).then_inc(s["expert_exp_ready"], 1)

            def gate_expert(t):
                act.wait_ge(s["expert_in_psum"], t + 1)
                if t >= 2:
                    act.wait_ge(s["cT_in_psum"], t - 1)
                nc.scalar.activation(es_t[:, t % 2, :], ps[:, 6 + t % 2, :], ACT.Silu
                                     ).then_inc(s["expert_silu_ready"], 1)

            hidden_high(G * FM - 1)

            def combined_high(t):
                act.wait_ge(s["cT_in_psum"], t + 1)
                if t >= 2:
                    act.wait_ge(s["out_in_psum"], t - 1)
                nc.scalar.copy(cT_hi[:, t % 2, :, :].rearrange("p c t -> p (c t)"), ps[:, 4 + t % 2, :]
                               ).then_inc(s["cT_hi_ready"], 1)

            gate_expert(0)
            gate_expert(1)
            combined_high(0)
            for t in range(NT):
                if t + 1 < NT:
                    combined_high(t + 1)
                if t + 2 < NT:
                    gate_expert(t + 2)
                if t == 1:
                    ranks_out(1)

        @blk.vector
        def _(dve):
            n = [0]

            def note(ins):
                n[0] += 1
                ins.then_inc(s["vector_done"], 1)

            def link(ins):
                note(ins)
                dve.wait_ge(s["vector_done"], n[0])

            V = nc.vector

            def stats1(b):
                link(V.bn_stats(stat1[:, b, :], x_sb[:, b, :]))
                V.bn_aggr(mv1[:, b, :], stat1[:, b, :]).then_inc(s["moments1_ready"], 1)

            def xhat(b):
                if b >= 2:
                    dve.wait_ge(s["xT_in_psum"], b - 1)
                V.tensor_scalar(xh[:, b % 2, :], x_sb[:, b, :], mv1[:, b, 0:1], rstd1[:, b:b + 1], ALU.subtract,
                                ALU.mult).then_inc(s["xhat_ready"], 1)

            def kv_products(b):
                if b >= 2:
                    dve.wait_ge(s["conv_in_psum"], 2 * KC * (b - 1))
                for c in range(KC):
                    src = kk[:, c, 2 * b:2 * b + 2, :, 0:HD]
                    V.tensor_tensor(kv[:, b % 2, c, :, :, :, :].rearrange("p h b d i -> p (h b) d i"),
                                    view(src, [[KW, 2 * B], [0, ND], [1, HD]]),
                                    view(src, [[KW, 2 * B], [1, ND], [1, HD]]), ALU.mult).then_inc(s["kv_ready"], 1)

            def q_cols(b):
                dve.wait_ge(s["Q_in_psum"], b + 1)
                if b >= 2:
                    dve.wait_ge(s["scoresT_in_psum"], 2 * (b - 1))
                for c in range(KC):
                    for e in range(2):
                        V.tensor_scalar(qT[:, b % 2, c, e, :], Q_ps[:, c, :], bq_col[:, c:c + 1],
                                        head_sel[:, e:e + 1], ALU.add, ALU.mult).then_inc(s["qT_ready"], 1)

            def v_rows(b):
                dve.wait_ge(s["V_in_psum"], b + 1)
                if b >= 2:
                    dve.wait_ge(s["PV_in_psum"], RG * (b - 1))
                V.tensor_tensor(vext[:, b % 2, :, 0:DH], V_ps.rearrange("p (h e) -> p h e", h=H),
                                bv_row[:, :].rearrange("p (h e) -> p h e", h=H), ALU.add).then_inc(s["values_ready"], 1)

            def row_max(b, r):
                if r == 0:
                    dve.wait_ge(s["scores_in_psum"], b + 1)
                if b >= 1 and r != 1:
                    dve.wait_ge(s["shift_ready"], 3 * (b - 1) + (1, 0, 2, 3)[r])
                V.tensor_reduce(negmax[:, r, :, :].rearrange("p t e -> p (t e)"),
                                sc_ps[:, r, :].rearrange("p (h k) -> p h k", k=P), AX.X, ALU.max, negate=True
                                ).then_inc(s["max_ready"], 1)
                if r == 1:
                    dve.wait_ge(s["max_ready"], RG * b + 2)
                    if b == 0:
                        dve.wait_ge(s["consts_ready"], 3)
                    else:
                        dve.wait_ge(s["scoresT_in_psum"], 2 * (b - 1) + 1)
                    V.tensor_tensor(shift[:, r, :, :], bc(ident_bf[:, :], 1, KC * 2),
                                    bc(negmax[:, r, :, :].rearrange("p t e -> p (t e)"), 2, P), ALU.mult
                                    ).then_inc(s["shift1_ready"], 1)

            def attn_norm(b):
                dve.wait_ge(s["PV_in_psum"], RG * (b + 1))
                link(V.reciprocal(rsum[:, :], PV_ps[:, :, DH]))
                if b >= 1:
                    dve.wait_ge(s["avT_in_psum"], b)
                V.tensor_tensor(av[:, :].rearrange("p (h e) -> p h e", h=H), PV_ps[:, :, 0:DH],
                                bc(rsum[:, :], 2, DH), ALU.mult).then_inc(s["av_ready"], 1)

            def attn_res(b):
                dve.wait_ge(s["wo_in_psum"], b + 1)
                dve.wait_ge(s["x_bias_ready"], b + 1)
                V.tensor_tensor(res[:, :], wo_ps, xb_sb[:, b, :], ALU.add).then_inc(s["residual2_ready"], 1)
                dve.wait_ge(s["residual2_ready"], b + 1)
                link(V.bn_stats(stat2[:, :], res[:, :]))
                link(V.bn_aggr(mv2[:, :], stat2[:, :]))
                V.tensor_scalar(var2[:, :], mv2[:, 1:2], EPS, None, ALU.add).then_inc(s["var2_ready"], 1)

            def attn_out(b):
                dve.wait_ge(s["rstd2_ready"], b + 1)
                V.tensor_scalar(x1[:, b, :], res[:, :], mv2[:, 0:1], rstd2[:, :], ALU.subtract, ALU.mult
                                ).then_inc(s["x1_ready"], 1)

            def skip_weights(g):
                dve.wait_ge(s[f"loaded_toep{g}"], 16)
                for h in range(4 * g, 4 * g + 4):
                    V.scalar_tensor_tensor(toep[:, h, 0:P], anti[:, :], skip_row[:, h:h + 1], toep[:, h, 0:P],
                                           ALU.mult, ALU.add).then_inc(s["toep_ready"], 1)

            def variances(b0, b1):
                for b in range(b0, b1):
                    stats1(b)
                dve.wait_ge(s["moments1_ready"], b1)
                V.tensor_scalar(var1[:, b0:b1], mv1[:, b0:b1, 1], EPS, None, ALU.add).then_inc(s["var1_ready"], 1)

            dve.wait_ge(s["loaded_x0"], 16)
            variances(0, 2)
            dve.wait_ge(s["identity_ready"], 1)
            for e in range(2):
                link(V.tensor_reduce(head_sel[:, e:e + 1],
                                     ident[:, :].rearrange("p (g e i) -> p g e i", g=RG, e=2)[:, :, e, :],
                                     AX.XY, ALU.add))
            link(V.tensor_scalar(head_sel[:, :], head_sel[:, :], float(DH) ** -0.5, None, ALU.mult))
            dve.wait_ge(s["rstd1_ready"], 1)
            xhat(0)
            xhat(1)
            dve.wait_ge(s["loaded_cols"], 16)
            q_cols(0)
            dve.wait_ge(s["loaded_rows"], 16)
            v_rows(0)

            for b in range(B):
                if b >= 1:
                    attn_norm(b - 1)
                for r in range(RG):
                    row_max(b, r)
                if b == 0:
                    dve.wait_ge(s["identity_ready"], 2)
                    skip_weights(0)
                    dve.wait_ge(s["loaded_ctx0"], 16)
                    kv_products(0)
                    dve.wait_ge(s["loaded_x1"], 16)
                    variances(2, B)
                if b + 1 < B:
                    if b == 1:
                        dve.wait_ge(s["loaded_ctx1"], 16)
                    kv_products(b + 1)
                if b % 2 == 0 and b // 2 + 1 < TG4:
                    skip_weights(b // 2 + 1)
                if b >= 1:
                    attn_res(b - 1)
                if b + 1 < B:
                    q_cols(b + 1)
                if b >= 1:
                    attn_out(b - 1)
                if b + 2 < B:
                    if b == 0:
                        dve.wait_ge(s["rstd1_ready"], 2)
                    xhat(b + 2)
                if b + 1 < B:
                    v_rows(b + 1)

            def cross_products(b, c):
                if c == 0:
                    dve.wait_ge(s["queries_ready"], 3 * (b + 1))
                    if b == 0:
                        dve.wait_ge(s["Y_wrapped"], KC * B)
                    if b >= 2:
                        dve.wait_ge(s["sum_in_psum"], b - 1)
                row = B * ND * YW
                yb = Y[:, c, :, b, :, :]
                q0 = qq[:, b % 2, c, :, :]
                V.tensor_tensor(z[b % 2][:, c, 0:ND, :, :], view(yb, [[YW, ND], [row, H], [1, HD]], WR),
                                view(q0, [[1, ND], [QW, H], [1, HD]], WR), ALU.mult).then_inc(s["terms_ready"], 1)
                V.tensor_tensor(z[b % 2][:, c, ND:TK, :, :], view(yb, [[YW - 1, WR], [row, H], [1, HD]], YW + WR - 1),
                                view(q0, [[-1, WR], [QW, H], [1, HD]], WR - 1), ALU.mult).then_inc(s["terms_ready"], 1)

            def cross_res(b):
                dve.wait_ge(s["sum_in_psum"], b + 1)
                r = res2[:, b % 2, :]
                link(V.tensor_tensor(r, ps[:, 4 + b % 2, 0:D], x1[:, b, :], ALU.add))
                link(V.bn_stats(stat3[:, :], r))
                link(V.bn_aggr(mv3[:, :], stat3[:, :]))
                V.tensor_scalar(var3[:, :], mv3[:, 1:2], EPS, None, ALU.add).then_inc(s["var3_ready"], 1)

            def cross_out(b):
                dve.wait_ge(s["rstd3_ready"], b + 1)
                V.tensor_scalar(x2[:, b, :], res2[:, b % 2, :], mv3[:, 0:1], rstd3[:, :], ALU.subtract, ALU.mult
                                ).then_inc(s["x2_ready"], 1)

            attn_norm(B - 1)
            for c in range(KC):
                cross_products(0, c)
            for c in range(KC):
                cross_products(1, c)
            attn_res(B - 1)
            attn_out(B - 1)
            for b in range(B):
                cross_res(b)
                if b + 2 < B:
                    cross_products(b + 2, 0)
                cross_out(b)
                if b + 2 < B:
                    cross_products(b + 2, 1)

            def hidden(u):
                dve.wait_ge(s["silu_ready"], u + 1)
                V.tensor_tensor(gs[:, u % 3, :], ps[:, 3 + 2 * (u % 3), :], gs[:, u % 3, :], ALU.mult
                                ).then_inc(s["hidden_ready"], 1)
                if u >= 1 and u - 1 not in pool_units:
                    hidden_low(u - 1)

            def hidden_low(u):
                dve.wait_ge(s["hidden_hi_ready"], u + 1)
                g, m = divmod(u, FM)
                V.tensor_tensor(hT_lo[:, m, 512 * g:512 * (g + 1)], gs[:, u % 3, :],
                                hT_hi[:, m, 512 * g:512 * (g + 1)], ALU.subtract).then_inc(s["hidden_lo_ready"], 1)

            def best_keys(t):
                dve.wait_ge(s["route_scores_ready"], t // 4 + 1)
                note(V.max(v8[:, t, 0, :], rt[:, t, 0, :]))
                link(V.max(v8[:, t, 1, :], rt[:, t, 1, :]))
                note(V.max_index(i8[:, t, 0, :], v8[:, t, 0, :], rt[:, t, 0, :]))
                link(V.max_index(i8[:, t, 1, :], v8[:, t, 1, :], rt[:, t, 1, :]))
                V.tensor_copy(f8[:, t, :, :], i8[:, t, :, :]).then_inc(s["best_keys_ready"], 1)

            dve.wait_ge(s["consts_ready"], 4)
            hidden(0)
            hidden(1)
            for i in range(NP, NW):
                w, hi, lo = wide[i]
                dve.wait_ge(s["weights_hi_ready"], i + 1)
                V.tensor_tensor(lo, w, hi, ALU.subtract).then_inc(s["ue_lo_ready"], 1)
            for t in range(NT):
                best_keys(t)
                if t >= 1:
                    hidden(t + 1)
            dve.wait_ge(s["best_keys_ready"], NT)
            link(V.tensor_tensor(pair[:, :, :, :], bc(v8[:, :, 0, :], 3, TK), bc(v8[:, :, 1, :], 2, TK), ALU.add))
            for t in range(NT):
                note(V.max(m8[:, t, :], pair[:, t, :, :].rearrange("p a b -> p (a b)")))
            dve.wait_ge(s["vector_done"], n[0])
            for t in range(NT):
                note(V.match_replace(pair_r[:, t, :, :].rearrange("p a b -> p (a b)"), m8[:, t, :],
                                     pair[:, t, :, :].rearrange("p a b -> p (a b)"), LOWEST))
            dve.wait_ge(s["vector_done"], n[0])
            hidden(9)
            V.tensor_tensor(ew[:, :, :, :].rearrange("p t a b -> p t (a b)"),
                            pair[:, :, :, :].rearrange("p t a b -> p t (a b)"), bc(m8[:, :, 0], 2, TK * TK),
                            ALU.subtract).then_inc(s["exp_arguments_ready"], 1)
            V.tensor_tensor(ex[:, :, :], rt[:, :, 0, 0:TK], bc(v8[:, :, 0, 0], 2, TK), ALU.subtract
                            ).then_inc(s["exp_arguments_ready"], 1)
            V.tensor_tensor(ey[:, :, :], rt[:, :, 1, :], bc(v8[:, :, 1, 0], 2, NK), ALU.subtract
                            ).then_inc(s["exp_arguments_ready"], 1)
            link(V.tensor_tensor(sel[:, :, :, :], pair_r[:, :, :, :], pair[:, :, :, :], ALU.not_equal))
            link(V.tensor_reduce(cnt[:, :, :], sel[:, :, :, :], AX.X, ALU.add))
            hidden(10)
            link(V.tensor_tensor(tmp[:, :, :, :], bc(f8[:, :, 0, :], 2, TK),
                                 view(iota_f[:, 0:TK], [[0, NT], [1, TK], [0, TK]]), ALU.is_equal))
            link(V.tensor_tensor(tmp[:, :, :, :], tmp[:, :, :, :], bc(cnt[:, :, :], 2, TK), ALU.mult))
            V.tensor_reduce(cx[:, :, :], tmp[:, :, :, :], AX.X, ALU.add).then_inc(s["counts_ready"], 1)
            dve.wait_ge(s["counts_ready"], 1)
            hidden(11)
            dve.wait_ge(s["expert_exp_ready"], 3)
            link(V.tensor_tensor(ew[:, :, :, :], ew[:, :, :, :], sel[:, :, :, :], ALU.mult))
            hidden(12)
            link(V.tensor_reduce(zs[:, :], ew[:, :, :, :], AX.XY, ALU.add))
            link(V.reciprocal(rz[:, :], zs[:, :]))
            V.tensor_tensor(ex[:, :, :], ex[:, :, :], bc(rz[:, :], 2, TK), ALU.mult).then_inc(s["ex_scaled"], 1)
            hidden(13)
            link(V.tensor_scalar(fx64[:, :, :], f8[:, :, 0, :], float(NK), None, ALU.mult))
            link(V.tensor_tensor(tmp[:, :, :, :], bc(fx64[:, :, :], 3, TK), bc(f8[:, :, 1, :], 2, TK), ALU.add))
            fl = "p t a b -> p (t a b)"
            link(V.scalar_tensor_tensor(tmp[:, :, :, :].rearrange(fl), tmp[:, :, :, :].rearrange(fl), float(NE - 1),
                                        ew[:, :, :, :].rearrange(fl), ALU.is_ge, ALU.mult))
            link(V.tensor_reduce(p511[:, :], tmp[:, :, :, :], AX.XY, ALU.add))
            link(V.tensor_tensor(p511[:, :], p511[:, :], rz[:, :], ALU.mult))
            def select(t):
                dve.wait_ge(s["rank_plus_count_ready"], t + 1)
                V.scalar_tensor_tensor(pd[:, t, :, :], pd[:, t, :, :], TK + 0.5, bc(ey[:, t, :], 1, TK),
                                       ALU.is_gt, ALU.mult).then_inc(s["selected_ready"], 1)

            def combine(t):
                dve.wait_ge(s["weighted_ready"], t + 1)
                link(V.tensor_copy(pd[:, t, TK - 1, NK - 1:NK], p511[:, t:t + 1]))
                dve.wait_ge(s["expert_silu_ready"], t + 1)
                V.tensor_tensor(es_t[:, t % 2, :], es_t[:, t % 2, :], pd[:, t, :, :].rearrange("p a b -> p (a b)"),
                                ALU.mult).then_inc(s["expert_weighted"], 1)

            hidden(14)
            select(0)
            hidden(15)
            hidden_low(G * FM - 1)
            select(1)
            def last_norm(t):
                dve.wait_ge(s["out_in_psum"], t + 1)
                r = res4[:, t % 2, :]
                link(V.tensor_tensor(r, ps[:, (0, 1, 3)[t % 3], 0:D], x2[:, t, :], ALU.add))
                link(V.bn_stats(stat4[:, :], r))
                link(V.bn_aggr(mv4[:, :], stat4[:, :]))
                V.tensor_scalar(var4[:, :], mv4[:, 1:2], EPS, None, ALU.add).then_inc(s["var4_ready"], 1)
                dve.wait_ge(s["rstd4_ready"], t + 1)
                if t >= 2:
                    dve.wait_ge(s["stored"], 16 * (t - 1))
                V.tensor_scalar(y_out[:, t % 2, :], r, mv4[:, 0:1], rstd4[:, :], ALU.subtract, ALU.mult
                                ).then_inc(s["y_ready"], 1)

            def combined_low(t):
                dve.wait_ge(s["cT_hi_ready"], t + 1)
                V.tensor_tensor(cT_lo[:, t % 2, :, :].rearrange("p c t -> p (c t)"), ps[:, 4 + t % 2, :],
                                cT_hi[:, t % 2, :, :].rearrange("p c t -> p (c t)"), ALU.subtract
                                ).then_inc(s["cT_lo_ready"], 1)

            combine(0)
            select(2)
            combine(1)
            combined_low(0)
            for t in range(NT):
                if t + 1 < NT:
                    combined_low(t + 1)
                if t + 2 < NT:
                    combine(t + 2)
                if t + 3 < NT:
                    select(t + 3)
                if t >= 1:
                    last_norm(t - 1)
            last_norm(NT - 1)

        @blk.tensor
        def _(pe):
            M = nc.tensor.matmul
            T = nc.tensor.transpose

            def x_transpose(b):
                pe.wait_ge(s["xhat_ready"], b + 1)
                if b >= 1:
                    pe.wait_ge(s["kT_ready"], KC * b)
                for c in range(KC):
                    last = T(xT_ps[:, c, :], xh[:, b % 2, c * P:(c + 1) * P], ident[:, :])
                last.then_inc(s["xT_in_psum"], 1)

            def split_products(dst, terms, start=True, stop=True):
                for i, (a_hi, a_lo, b_hi, b_lo) in enumerate(terms):
                    M(dst, a_lo, b_hi, start=(start and i == 0), stop=False)
                    M(dst, a_hi, b_hi, start=False, stop=False)
                    last = M(dst, a_hi, b_lo, start=False, stop=(stop and i == len(terms) - 1))
                return last

            def project_cols(b, w, dst):
                for c in range(KC):
                    cs = slice(c * P, (c + 1) * P)
                    for k in range(KC):
                        last = M(dst[:, c, :], w_sb[w][:, k, cs], xnT[:, b % 2, k, :], start=(k == 0),
                                 stop=(k == KC - 1))
                return last

            def project_keys(b):
                pe.wait_ge(s["xnT_ready"], KC * (b + 1))
                if b == 0:
                    pe.wait_ge(s["loaded_wk"], 16)
                project_cols(b, "k", K_ps).then_inc(s["K_in_psum"], 1)

            def project_queries(b):
                if b == 0:
                    pe.wait_ge(s["loaded_wq"], 16)
                else:
                    pe.wait_ge(s["values_ready"], b)
                project_cols(b, "q", Q_ps).then_inc(s["Q_in_psum"], 1)

            def project_values(b):
                if b == 0:
                    pe.wait_ge(s["loaded_wv"], 16)
                pe.wait_ge(s["qT_ready"], 2 * KC * (b + 1))
                if b < FIRST_SPLIT:
                    for k in range(KC):
                        last = M(V_ps, xnT[:, b % 2, k, :], w_sb["v"][:, k, :], start=(k == 0), stop=(k == KC - 1))
                else:
                    pe.wait_ge(s["xnT_lo_ready"], b - FIRST_SPLIT + 1)
                    if b == FIRST_SPLIT:
                        pe.wait_ge(s["wv_lo_ready"], 1)
                    last = split_products(V_ps, [(xnT_hi[:, b % 2, k, :], xnT_lo[:, b % 2, k, :], wv_hi[:, k, :],
                                                  wv_lo[:, k, :]) for k in range(KC)])
                last.then_inc(s["V_in_psum"], 1)

            def scores(b):
                pe.wait_ge(s["rounded_ready"], 2 * (b + 1))
                if b >= 1:
                    pe.wait_ge(s["exp_ready"], RG * b)
                for r in range(RG):
                    M(sc_ps[:, r, :], ident_bf[:, :], bc(mask_qk[:, :], 1, 4), start=True,
                      stop=False)
                for t in range(KC):
                    for e in range(2):
                        for r in range(RG):
                            i = 2 * t + e
                            last = M(sc_ps[:, r, i * P:(i + 1) * P], qT_bf[32 * r:32 * r + 32, t, e, :],
                                     kT_bf[32 * r:32 * r + 32, t, :], start=False, stop=(i == 3))
                last.then_inc(s["scores_in_psum"], 1)

            def scores_t(b, half):
                pe.wait_ge(s["shift_ready"], 3 * b + (1, 3)[half])
                pe.wait_ge(s["shift1_ready"], b + 1)
                if half == 0:
                    pe.wait_ge(s["kT_lo_ready"], b + 1)
                    pe.wait_ge(s["qT_lo_ready"], b + 1)
                rr = range(2 * half, 2 * half + 2)
                for r in rr:
                    M(sc_ps[:, r, :], ones_bf[:, :], shift[:, r, :, :].rearrange("p e q -> p (e q)"), start=True,
                      stop=False)
                for t in range(KC):
                    for r in rr:
                        rows = slice(32 * r, 32 * r + 32)
                        last = split_products(sc_ps[:, r, 2 * t * P:2 * (t + 1) * P], [
                            (kT_hi[rows, b % 2, t, :], kT_lo[rows, b % 2, t, :],
                             qT_hi[rows, b % 2, t, :, :].rearrange("p e q -> p (e q)"),
                             qT_lo[rows, b % 2, t, :, :].rearrange("p e q -> p (e q)"))], start=False,
                            stop=(t == KC - 1))
                last.then_inc(s["scoresT_in_psum"], 1)

            def values(b, r):
                pe.wait_ge(s["probs_ready"], RG * b + r + 1)
                pe.wait_ge(s["values_ready"], b + 1)
                if b == 0:
                    pe.wait_ge(s["ones_column_ready"], 1)
                if b >= 1:
                    pe.wait_ge(s["residual2_ready"], b)
                for t in range(KC):
                    for e in range(2):
                        h = t * HALF + 2 * r + e
                        last = M(PV_ps[:, h, :], pT[:, r, t, e, :], vext[:, b % 2, h, :], start=True, stop=True)
                last.then_inc(s["PV_in_psum"], 1)

            def out_project(b):
                pe.wait_ge(s["av_ready"], b + 1)
                if b == 0:
                    pe.wait_ge(s["loaded_wo"], 16)
                for c in range(KC):
                    last = T(avT_ps[:, c, :], av[:, c * P:(c + 1) * P], ident[:, :])
                last.then_inc(s["avT_in_psum"], 1)

            def out_project2(b):
                pe.wait_ge(s["avT_ready"], b + 1)
                for c in range(KC):
                    last = M(wo_ps, avT[:, c, :], w_sb["o"][:, c, :], start=(c == 0), stop=(c == KC - 1))
                last.then_inc(s["wo_in_psum"], 1)

            def conv(h, c):
                pe.wait_ge(s["kv_ready"], KC * (h // 2 + 1))
                if h % 4 == 0:
                    pe.wait_ge(s["toep_ready"], h + 4)
                i = KC * h + c
                if i >= 1:
                    pe.wait_ge(s["Y_ready"], i)
                for k in range(c + 1):
                    d = c - k
                    last = M(conv_ps, toep[:, h, d * P:(d + 1) * P],
                             kv[:, h // 2 % 2, k, h % 2, :, :, :].rearrange("p b d i -> p (b d i)"), start=(k == 0),
                             stop=(k == c))
                last.then_inc(s["conv_in_psum"], 1)

            def keep_warm(n, bank):
                for _ in range(n):
                    M(ps[:, bank, :], ones_bf[:, :], bc(ones_bf[:, :], 1, 4), start=True, stop=True)

            pe.wait_ge(s["consts_ready"], 1)
            keep_warm(WARM, 7)
            pe.wait_ge(s["identity_ready"], 1)
            x_transpose(0)
            project_keys(0)
            project_queries(0)
            project_values(0)
            pe.wait_ge(s["consts_ready"], 3)
            for b in range(B):
                scores(b)
                if b == 0:
                    x_transpose(1)
                    project_keys(1)
                else:
                    out_project(b - 1)
                    conv(2 * b, 0)
                    out_project2(b - 1)
                    if b + 1 < B:
                        project_keys(b + 1)
                scores_t(b, 0)
                if b + 1 < B:
                    project_queries(b + 1)
                else:
                    keep_warm(3, 5)
                scores_t(b, 1)
                if b == 0:
                    conv(0, 0)
                conv(2 * b, 1)
                values(b, 0)
                conv(2 * b + 1, 0)
                values(b, 1)
                conv(2 * b + 1, 1)
                values(b, 2)
                if b + 1 < B:
                    project_values(b + 1)
                else:
                    keep_warm(2, 5)
                values(b, 3)
                if b + 2 < B:
                    x_transpose(b + 2)
            def cross_queries(b):
                pe.wait_ge(s["x1_ready"], b + 1)
                if b >= 2:
                    pe.wait_ge(s["queries_ready"], 3 * (b - 1))
                for c in range(KC):
                    last = T(ps[:, 2 + b % 2, c * P:(c + 1) * P], x1[:, b, c * P:(c + 1) * P], ident[:, :])
                last.then_inc(s["x1T_in_psum"], 1)

            def cross_sum(b):
                pe.wait_ge(s["terms_paired"], KC * (b + 1))
                if b >= 2:
                    pe.wait_ge(s["x2_ready"], b - 1)
                for c in range(KC):
                    for t in range(TK - 1):
                        last = M(ps[:, 4 + b % 2, c * P:(c + 1) * P],
                                 z[b % 2][:, c, t, :, :].rearrange("p h j -> p (h j)"), ident[:, :],
                                 start=(t == 0), stop=(t == TK - 2))
                last.then_inc(s["sum_in_psum"], 1)

            def x2_transpose(b):
                pe.wait_ge(s["x2_ready"], b + 1)
                if b >= 1:
                    pe.wait_ge(s["x2T_ready"], 2 * b)
                for c in range(KC):
                    last = T(ps[:, 6, c * P:(c + 1) * P], x2[:, b, c * P:(c + 1) * P], ident[:, :])
                last.then_inc(s["x2T_in_psum"], 1)

            def route_query(b):
                pe.wait_ge(s["x2T_ready"], 2 * b + 1)
                if b >= 1:
                    pe.wait_ge(s["route_queries_ready"], 2 * b)
                else:
                    pe.wait_ge(s["loaded_wqr"], 16)
                for c in range(KC):
                    last = M(ps[:, 7, 0:P], wqr_sb[:, c, :], x2T[:, b % 2, c, :], start=(c == 0), stop=(c == KC - 1))
                last.then_inc(s["route_query_in_psum"], 1)

            pe.wait_ge(s["exp_ready"], RG * B)
            cross_queries(0)
            cross_queries(1)
            out_project(B - 1)
            out_project2(B - 1)

            for b in range(B):
                if b + 2 < B:
                    cross_queries(b + 2)
                cross_sum(b)
                if b >= 1:
                    x2_transpose(b - 1)
                if b >= 2:
                    route_query(b - 2)

            def routing(i):
                if i == 0:
                    pe.wait_ge(s["loaded_key"], 32)
                    pe.wait_ge(s["route_queries_ready"], 2 * B)
                for t in range(4 * i, 4 * i + 4):
                    for a in range(2):
                        c0 = (t % 4) * 2 * NK + a * NK
                        col = (a * NT + t) * P
                        last = M(ps[:, i, c0:c0 + NK], qm[:, col:col + P], key_sb[:, a, :], start=True, stop=True)
                last.then_inc(s["route_scores_in_psum"], 1)

            def gate_up(u, halves=(0, 1)):
                g, m = divmod(u, FM)
                if u == 0:
                    pe.wait_ge(s["weights_lo_ready"], 8)
                if m == 0:
                    pe.wait_ge(s["x2T_lo_ready"], TG * (g + 1))
                if u == 1:
                    pe.wait_ge(s["x2_ready"], B)
                if u == 2:
                    pe.wait_ge(s["route_queries_ready"], 2 * B)
                if u >= 3:
                    pe.wait_ge(s["hidden_ready"], u - 2)
                for a, (hi, lo) in enumerate(((gate_hi, gate_lo), (up_hi, up_lo))):
                    ms = slice(m * P, (m + 1) * P)
                    gt = slice(TG * g, TG * (g + 1))
                    if a not in halves:
                        continue
                    last = split_products(ps[:, 2 + 2 * (u % 3) + a, :], [
                        (hi[:, k, ms], lo[:, k, ms], x2T_hi[:, k, gt, :].rearrange("p b t -> p (b t)"),
                         x2T_lo[:, k, gt, :].rearrange("p b t -> p (b t)")) for k in range(KC)])
                if 1 in halves:
                    last.then_inc(s["gate_up_in_psum"], 1)

            gate_up(0)
            x2_transpose(B - 1)
            route_query(B - 2)
            gate_up(1, (0,))
            route_query(B - 1)
            gate_up(1, (1,))
            routing(0)
            routing(1)
            def rank_sum(i):
                pe.wait_ge(s["rank_rows_ready"], 4 * TK * (i + 1))
                if i == 0:
                    pe.wait_ge(s["route_scores_ready"], 1)
                for k in range(TK):
                    last = M(ps[:, 2 * i, 0:4 * NK], ident_bf[:, :], rk[:, 4 * i:4 * i + 4, k, :], start=(k == 0),
                             stop=(k == TK - 1))
                last.then_inc(s["rank_in_psum"], 1)

            for u in range(2, G * FM):
                gate_up(u)
                if u == RANKS_AT:
                    rank_sum(0)

            def expert_in(t):
                if t >= 2:
                    pe.wait_ge(s["expert_silu_ready"], t - 1)
                last = split_products(ps[:, 6 + t % 2, :], [
                    (x2T_hi[:, k, t, :], x2T_lo[:, k, t, :], deT_hi[:, k, :], deT_lo[:, k, :]) for k in range(KC)])
                last.then_inc(s["expert_in_psum"], 1)

            def expert_transpose(t):
                pe.wait_ge(s["expert_weighted"], t + 1)
                if t >= 2:
                    pe.wait_ge(s["cT_lo_ready"], t - 1)
                for e in range(EC):
                    last = T(ps[:, 4 + t % 2, e * P:(e + 1) * P], es_t[:, t % 2, e * P:(e + 1) * P], ident[:, :])
                last.then_inc(s["cT_in_psum"], 1)

            pe.wait_ge(s["hidden_ready"], G * FM - 1)
            pe.wait_ge(s["route_scores_ready"], 2)
            pe.wait_ge(s["deT_lo_ready"], 1)
            expert_in(0)
            expert_in(1)
            pe.wait_ge(s["weights_lo_ready"], NP)
            pe.wait_ge(s["ue_lo_ready"], NW - NP)
            wait_low(pe, FM - 1)
            o_banks = (0, 1, 3)
            out_ps = [ps[:, o_banks[t % 3], 0:D] for t in range(NT)]

            def down(t):
                if t == TG:
                    wait_low(pe, G * FM - 1)
                if t >= 3:
                    pe.wait_ge(s["y_ready"], t - 2)
                ts = slice(t * P, (t + 1) * P)
                split_products(out_ps[t], [(hT_hi[:, m, ts], hT_lo[:, m, ts], down_hi[:, m, :], down_lo[:, m, :])
                                           for m in range(FM)], stop=False)

            down(0)
            down(1)
            expert_transpose(0)
            for t in range(NT):
                if t + 1 < NT:
                    expert_transpose(t + 1)
                    if t + 2 < NT:
                        expert_in(t + 2)
                    if t == 1:
                        rank_sum(1)
                    if t > 0:
                        down(t + 1)
                pe.wait_ge(s["cT_lo_ready"], t + 1)
                last = split_products(out_ps[t], [(cT_hi[:, t % 2, e, :], cT_lo[:, t % 2, e, :], ue_hi[:, e, :],
                                                   ue_lo[:, e, :]) for e in range(EC)], start=False)
                last.then_inc(s["out_in_psum"], 1)



def kernel(**inputs):
    import numpy as np
    import concourse.bacc as bacc
    from concourse.bass_utils import run_bass_kernel_spmd

    names = ['x', 'ctx_2048', 'L0_attn_Wq', 'L0_attn_Wk', 'L0_attn_Wv', 'L0_attn_Wo', 'L0_xattn_ssm_kernel',
             'L0_ffn_W_q', 'L0_ffn_keys', 'L0_ffn_down_embed', 'L0_ffn_up_embed', 'L0_ffn_gate_w', 'L0_ffn_up_w',
             'L0_ffn_down_w']
    data = {name: np.ascontiguousarray(inputs[name]) for name in names}
    taps = data['L0_xattn_ssm_kernel']
    data['L0_xattn_ssm_kernel'] = np.concatenate([np.zeros((taps.shape[0], 127), taps.dtype), taps], axis=1)
    data['L0_ffn_down_embed'] = np.ascontiguousarray(data['L0_ffn_down_embed'].T)
    H, ND = taps.shape[0], 5
    B, S, D = data['ctx_2048'].shape
    ctx = data['ctx_2048'].reshape(B, H, S // H, D // 128, 128)[:, :, :, :, ::-1]
    ctx = np.concatenate([ctx, ctx[:, :, :ND - 1]], axis=2)
    data['ctx_2048'] = np.ascontiguousarray(ctx.transpose(4, 3, 1, 0, 2))
    per_channel = [inputs[f'L0_attn_{n}'] for n in ('ln_g', 'ln_b', 'bq', 'bk')]
    data['columns'] = np.ascontiguousarray(np.stack([v.reshape(-1, 128).T for v in per_channel], axis=1))
    data['rows'] = np.concatenate([inputs[n].reshape(-1) for n in ('L0_attn_bv', 'L0_attn_bo', 'L0_xattn_D')])
    nc = bacc.Bacc("TRN2", target_bir_lowering=False, num_devices=1)
    arrays = {f"in_{name}": a for name, a in data.items()}
    args = [nc.dram_tensor(name, a.shape, mybir.dt.from_np(a.dtype), kind="ExternalInput").ap()
            for name, a in arrays.items()]
    shape = tuple(inputs['x'].shape)
    args.append(nc.dram_tensor("out_0", shape, mybir.dt.float32, kind="ExternalOutput").ap())
    decoder_layer(nc, *args)
    r = run_bass_kernel_spmd(nc, [arrays], core_ids=[0])
    return r.results[0]["out_0"]
```
